# Optimizing a Trainium2 kernel written in Bass

```python
import numpy as np
import jax
import jax.numpy as jnp

def _softmax(x, axis=-1):
    return jax.nn.softmax(x, axis=axis)
def _gelu(x):
    return jax.nn.gelu(x, approximate=True)
def _silu(x):
    return jax.nn.silu(x)
def _sigmoid(x):
    return jax.nn.sigmoid(x)
def _layernorm(x, axis=-1, eps=1e-5):
    m = jnp.mean(x, axis=axis, keepdims=True)
    v = jnp.var(x, axis=axis, keepdims=True)
    return (x - m) / jnp.sqrt(v + eps)
def _scatter_add(tgt, idx, src, axis=0):
    return tgt.at[idx].add(src)
def _segment_sum(src, seg, n):
    return jax.ops.segment_sum(src, seg, n)

kernel_name = 'mk_adj_seq_d1_adj_512_49ddcf'

def setup_inputs(seed: int = 0):
    np.random.seed(seed)
    _w = jnp.asarray
    def _rec_inputs():
        import jax
        import jax.numpy as jnp
        _gk = jax.random.key(seed)
        x = -0.0005207 + 1.001 * jax.random.normal(jax.random.fold_in(_gk, 1), (128, 64, 512), jnp.float32)
        _w = (1.0 + jnp.arange(64, dtype=jnp.float32)) ** -0.5
        _w = _w / _w.mean()
        _pij = jnp.clip(0.0625 * _w[:, None] * _w[None, :], 0.0, 1.0)
        _a = jax.random.uniform(jax.random.fold_in(_gk, 2), (128, 64, 64)) < _pij
        adj = _a
        return x, adj
    x, adj = _rec_inputs()
    def _L0_gnn_setup():
        import jax, jax.numpy as jnp
        import numpy as np
        HIDDEN = 512
        HEADS = 8
        HEAD_DIM = HIDDEN // HEADS
        D_FF = 4 * HIDDEN
        NEG = -1000000000.0

        def _layernorm(x, g, b, eps=1e-05):
            mu = jnp.mean(x, axis=-1, keepdims=True)
            var = jnp.var(x, axis=-1, keepdims=True)
            return (x - mu) * jax.lax.rsqrt(var + eps) * g + b
        key = jax.random.key(seed)
        ks = jax.random.split(key, 16)
        B, S = (2, 2048)
        s = 1.0 / np.sqrt(HIDDEN)
        inp = {'x': jax.random.normal(ks[0], (B, S, HIDDEN), dtype=jnp.float32), 'adj_mask': jax.random.bernoulli(ks[1], 0.5, (B, S, S)), 'ln1_g': jnp.ones((HIDDEN,), jnp.float32), 'ln1_b': jnp.zeros((HIDDEN,), jnp.float32), 'ln2_g': jnp.ones((HIDDEN,), jnp.float32), 'ln2_b': jnp.zeros((HIDDEN,), jnp.float32), 'Wq': jax.random.uniform(ks[2], (HIDDEN, HIDDEN), jnp.float32, -s, s), 'bq': jnp.zeros((HIDDEN,), jnp.float32), 'Wk': jax.random.uniform(ks[3], (HIDDEN, HIDDEN), jnp.float32, -s, s), 'bk': jnp.zeros((HIDDEN,), jnp.float32), 'Wv': jax.random.uniform(ks[4], (HIDDEN, HIDDEN), jnp.float32, -s, s), 'bv': jnp.zeros((HIDDEN,), jnp.float32), 'Wo': jax.random.uniform(ks[5], (HIDDEN, HIDDEN), jnp.float32, -s, s), 'bo': jnp.zeros((HIDDEN,), jnp.float32), 'W1': jax.random.uniform(ks[6], (HIDDEN, D_FF), jnp.float32, -s, s), 'b1': jnp.zeros((D_FF,), jnp.float32), 'W2': jax.random.uniform(ks[7], (D_FF, HIDDEN), jnp.float32, -1.0 / np.sqrt(D_FF), 1.0 / np.sqrt(D_FF)), 'b2': jnp.zeros((HIDDEN,), jnp.float32)}
        return inp
    _L0_gnn_all = _L0_gnn_setup()
    _L0_gnn_in = {k: v for k, v in _L0_gnn_all.items() if k in ('ln1_g', 'ln1_b', 'ln2_g', 'ln2_b', 'Wq', 'bq', 'Wk', 'bk', 'Wv', 'bv', 'Wo', 'bo', 'W1', 'b1', 'W2', 'b2', )}
    del _L0_gnn_all

    return {
        "x": x,
        "adj": adj,
        "L0_gnn_ln1_g": _L0_gnn_in["ln1_g"],
        "L0_gnn_ln1_b": _L0_gnn_in["ln1_b"],
        "L0_gnn_ln2_g": _L0_gnn_in["ln2_g"],
        "L0_gnn_ln2_b": _L0_gnn_in["ln2_b"],
        "L0_gnn_Wq": _L0_gnn_in["Wq"],
        "L0_gnn_bq": _L0_gnn_in["bq"],
        "L0_gnn_Wk": _L0_gnn_in["Wk"],
        "L0_gnn_bk": _L0_gnn_in["bk"],
        "L0_gnn_Wv": _L0_gnn_in["Wv"],
        "L0_gnn_bv": _L0_gnn_in["bv"],
        "L0_gnn_Wo": _L0_gnn_in["Wo"],
        "L0_gnn_bo": _L0_gnn_in["bo"],
        "L0_gnn_W1": _L0_gnn_in["W1"],
        "L0_gnn_b1": _L0_gnn_in["b1"],
        "L0_gnn_W2": _L0_gnn_in["W2"],
        "L0_gnn_b2": _L0_gnn_in["b2"],
    }

def reference(x, adj, L0_gnn_ln1_g, L0_gnn_ln1_b, L0_gnn_ln2_g, L0_gnn_ln2_b, L0_gnn_Wq, L0_gnn_bq, L0_gnn_Wk, L0_gnn_bk, L0_gnn_Wv, L0_gnn_bv, L0_gnn_Wo, L0_gnn_bo, L0_gnn_W1, L0_gnn_b1, L0_gnn_W2, L0_gnn_b2):
    import jax
    import jax.numpy as jnp
    def _L0_gnn_ref(x, adj_mask, ln1_g, ln1_b, ln2_g, ln2_b, Wq, bq, Wk, bk, Wv, bv, Wo, bo, W1, b1, W2, b2):
        import jax, jax.numpy as jnp
        import numpy as np
        HIDDEN = 512
        HEADS = 8
        HEAD_DIM = HIDDEN // HEADS
        D_FF = 4 * HIDDEN
        NEG = -1000000000.0

        def _layernorm(x, g, b, eps=1e-05):
            mu = jnp.mean(x, axis=-1, keepdims=True)
            var = jnp.var(x, axis=-1, keepdims=True)
            return (x - mu) * jax.lax.rsqrt(var + eps) * g + b
        B, S, H = x.shape
        nx = _layernorm(x, ln1_g, ln1_b)
        q = (nx @ Wq + bq).reshape(B, S, HEADS, HEAD_DIM)
        k = (nx @ Wk + bk).reshape(B, S, HEADS, HEAD_DIM)
        v = (nx @ Wv + bv).reshape(B, S, HEADS, HEAD_DIM)
        scores = jnp.einsum('bqhd,bkhd->bhqk', q, k) / np.sqrt(HEAD_DIM)
        scores = jnp.where(adj_mask[:, None, :, :], scores, NEG)
        attn = jax.nn.softmax(scores, axis=-1)
        out = jnp.einsum('bhqk,bkhd->bqhd', attn, v).reshape(B, S, H)
        out = out @ Wo + bo
        x = x + out
        nx = _layernorm(x, ln2_g, ln2_b)
        mlp = jax.nn.gelu(nx @ W1 + b1, approximate=False) @ W2 + b2
        return x + mlp

    x = _L0_gnn_ref(x, adj, L0_gnn_ln1_g, L0_gnn_ln1_b, L0_gnn_ln2_g, L0_gnn_ln2_b, L0_gnn_Wq, L0_gnn_bq, L0_gnn_Wk, L0_gnn_bk, L0_gnn_Wv, L0_gnn_bv, L0_gnn_Wo, L0_gnn_bo, L0_gnn_W1, L0_gnn_b1, L0_gnn_W2, L0_gnn_b2)
    return x


_drawn_inputs = setup_inputs


def setup_inputs(seed=0):
    import zlib

    import numpy as np

    out = dict(_drawn_inputs(seed))
    spreads = {'L0_gnn_ln1_g': (1.0, 0.2),
     'L0_gnn_ln1_b': (0.0, 0.1),
     'L0_gnn_ln2_g': (1.0, 0.2),
     'L0_gnn_ln2_b': (0.0, 0.409),
     'L0_gnn_bq': (0.0, 0.8),
     'L0_gnn_bk': (0.0, 0.8),
     'L0_gnn_bv': (0.0, 0.1),
     'L0_gnn_bo': (0.0, 0.1),
     'L0_gnn_b1': (0.0, 0.1),
     'L0_gnn_b2': (0.0, 0.1)}
    factors = {}
    for name, (base, spread) in spreads.items():
        noise = np.random.default_rng([zlib.crc32(name.encode()), seed]).standard_normal(out[name].shape)
        drawn = base * np.exp(spread * noise) if base else spread * noise
        out[name] = jnp.asarray(drawn.astype(out[name].dtype))
    for name, factor in factors.items():
        out[name] = (out[name] * factor).astype(out[name].dtype)
    return out
```

```python
from contextlib import ExitStack

import concourse.bass as bass
from concourse import mybir

F32 = mybir.dt.float32
F32R = mybir.dt.float32r
U8 = mybir.dt.uint8
ALU = mybir.AluOpType
ACT = mybir.ActivationFunctionType
AX = mybir.AxisListType

P = 128
GRAPHS, NODES, HID = 128, 64, 512
HEADS = 8
HD = HID // HEADS
FF = 4 * HID
TOKENS = GRAPHS * NODES
KC = HID // P
FC = FF // P
TILES = 4
GT = TILES * P
NG = TOKENS // GT
EPS = 1e-5
SCALE = HD ** -0.5
NEG = -1.0e9 / SCALE

UNITS = 3 * KC
ORDER = [("S", 0), ("U", 0), ("U", 1), ("S", 1), ("U", 2), ("P", 0), ("U", 3), ("S", 2), ("O", 0), ("U", 4),
         ("P", 1), ("U", 5), ("S", 3), ("W", 0), ("U", 6), ("O", 1), ("P", 2), ("U", 7), ("W", 1), ("O", 2),
         ("U", 8), ("P", 3), ("U", 9), ("W", 2), ("U", 10), ("O", 3), ("U", 11),
         ("T", 0), ("T", 1), ("T", 2), ("T", 3), ("W", 3)]
LIN = 4


def kinds_of(g):
    if not isinstance(g, int):
        return "SUPOWT"
    return "SPOW" * (g >= 0) + "U" * (0 <= g + 1 < NG) + "T" * (g + 2 < NG)


def order_of(g):
    return [(k, n) for k, n in ORDER if k in kinds_of(g)]


def lin_uses(g):
    return [(g, k, n) for k, n in order_of(g) if k in "UTOW"]


def ring_place(g, kind, n):
    if isinstance(g, int):
        uses = [u for i in range(-2, g + 1) for u in lin_uses(i)]
        at = uses.index((g, kind, n))
        return at % LIN, uses[at - LIN] if at >= LIN else None
    uses = lin_uses(g)
    at = [u[1:] for u in uses].index((kind, n))
    assert len(uses) % LIN == 0 and len(lin_uses(-2) + lin_uses(-1) + lin_uses(0)) % LIN == 0
    return at % LIN, uses[at - LIN] if at >= LIN else (g - 1, *uses[at - LIN][1:])


def bank_of(g, kind, n):
    return ring_place(g, kind, n)[0]


def wait(eng, sem, value):
    if not isinstance(value, int) or value > 0:
        eng.wait_ge(sem, value)


def wait_apart(eng, sem, value, passed):
    wait(eng, sem, value)
    if not isinstance(value, int):
        eng.sem_inc(passed, 1)


def split3(pe, out, lhs, rhs, first, last):
    pe.matmul(out, lhs[1], rhs[0], start=first, stop=False)
    pe.matmul(out, lhs[0], rhs[1], start=False, stop=False)
    return pe.matmul(out, lhs[0], rhs[0], start=False, stop=last)


def attention_phase(nc, ins, x1_dram):
    x_dram, adj, ln_g, ln_b, wq, bq, wk, bk, wv, bv, wo, bo = ins
    x_groups = x_dram.rearrange("(g t p) n -> g p t n", t=TILES, p=P)
    x_tiles = x_dram.rearrange("(n p) d -> n p d", p=P)
    x1_tiles = x1_dram.rearrange("(n p) d -> n p d", p=P)
    adj_groups = adj.rearrange("(g t a) q k -> g (a q) t k", t=TILES, a=2)

    with ExitStack() as ctx:
        def sb(name, shape, dt=F32):
            return ctx.enter_context(nc.sbuf_tensor(name, shape, dt))

        def sem(name):
            return ctx.enter_context(nc.semaphore(name))

        w_hi = [sb(f"w{c}_hi", [P, KC, HID], F32R) for c in "qkvo"]
        w_lo = [sb(f"w{c}_lo", [P, KC, HID], F32R) for c in "qkvo"]
        nxT_hi = sb("nxT_hi", [P, KC, GT], F32R)
        nxT_lo = sb("nxT_lo", [P, KC, GT], F32R)
        nxT = sb("nxT", [P, 2, GT])
        x = [sb(f"x{i}", [P, TILES, HID]) for i in range(2)]
        qT = [sb(f"qT{i}", [P, KC, GT]) for i in range(2)]
        kT = [sb(f"kT{i}", [P, TILES, KC, 2 * P]) for i in range(2)]
        v = [sb(f"v{i}", [P, TILES, HID]) for i in range(2)]
        scores = sb("scores", [P, 2, HEADS, NODES])
        expd = sb("expd", [P, 2, HEADS, NODES])
        prob = sb("prob", [P, 2, HEADS, P])
        probT = sb("probT", [P, 2, HEADS * P])
        attT_hi = sb("attT_hi", [P, 2, HID], F32R)
        attT_lo = sb("attT_lo", [P, 2, HID], F32R)
        xres = sb("xres", [P, 2, HID])
        mask = sb("mask", [P, 2, TILES, NODES], U8)
        bv_all = sb("bv_all", [P, HID])
        bo_all = sb("bo_all", [P, HID])
        ident = sb("ident", [P, P])
        cols = sb("cols", [P, 4, KC])
        stats = sb("stats", [P, TILES, 6])
        moments = sb("moments", [P, TILES, 2])
        var_eps = sb("var_eps", [P, TILES])
        rstd = sb("rstd", [P, TILES])
        minus_half = sb("minus_half", [P, TILES])
        row_max = sb("row_max", [P, HEADS])
        row_sum = sb("row_sum", [P, HEADS])
        row_inv = sb("row_inv", [P, HEADS])

        lin = [ctx.enter_context(nc.psum_tensor(f"lin{i}", [P, GT], F32)) for i in range(LIN)]
        ps_scores = ctx.enter_context(nc.psum_tensor("ps_scores", [P, HEADS, P], F32))
        ps_probT = ctx.enter_context(nc.psum_tensor("ps_probT", [P, HEADS * P], F32))

        raw = [qT[1][:, :, :], v[1][:, :, :], probT[:, :, :].rearrange("p a (b n) -> p (a b) n", n=HID),
               qT[1][:, :, :]]

        x_loaded = [sem(f"x_loaded{i}") for i in range(2)]
        mask_loaded = [sem(f"mask_loaded{i}") for i in range(2)]
        xres_loaded = [sem(f"xres_loaded{i}") for i in range(2)]
        x1_stored = [sem(f"x1_stored{i}") for i in range(2)]
        w_loaded = [sem(f"w{c}_loaded") for c in "qkvo"]
        consts_loaded = sem("consts_loaded")
        w_hi_done, w_lo_done = sem("w_hi_done"), sem("w_lo_done")
        filled, ident_done, zeroed = sem("filled"), sem("ident_done"), sem("zeroed")
        stats_done, moments_done, var_done = sem("stats_done"), sem("moments_done"), sem("var_done")
        rstd_done, zn_done, t_done = sem("rstd_done"), sem("zn_done"), sem("t_done")
        nx_done, nx_hi_done, nx_split = sem("nx_done"), sem("nx_hi_done"), sem("nx_split")
        u_done, q_done, k_done, v_done = sem("u_done"), sem("q_done"), sem("k_done"), sem("v_done")
        s_done, neg_filled, masked, max_done = sem("s_done"), sem("neg_filled"), sem("masked"), sem("max_done")
        shifted, exp_done, sum_done, inv_done = sem("shifted"), sem("exp_done"), sem("sum_done"), sem("inv_done")
        prob_done, pt_done, probT_done = sem("prob_done"), sem("pt_done"), sem("probT_done")
        o_done, att_hi_done, att_split = sem("o_done"), sem("att_hi_done"), sem("att_split")
        mask_passed, fill_passed, stats_passed = sem("mask_passed"), sem("fill_passed"), sem("stats_passed")
        proj_done, xres_biased, x1_done = sem("proj_done"), sem("xres_biased"), sem("x1_done")

        block = ctx.enter_context(nc.Block())

        @block.sync
        def _(sp):
            def load_x(g, par):
                wait(sp, t_done, KC * (g - 1))
                sp.dma_start(x[par][:, :, :], x_groups[g]).then_inc(x_loaded[par], 16)

            def load_mask(g, par):
                with nc.allow_non_contiguous_dma(reason="rows of 64 flags"):
                    sp.dma_start(mask[:, par], adj_groups[g]).then_inc(mask_loaded[par], 16)

            def load_xres(g, t):
                wait(sp, x1_stored[t % 2], 16 * (2 * g + t // 2))
                sp.dma_start(xres[:, t % 2], x_tiles[g * TILES + t]).then_inc(xres_loaded[t % 2], 16)

            def store_x1(g, t):
                sp.wait_ge(x1_done, TILES * g + t + 1)
                sp.dma_start(x1_tiles[g * TILES + t], xres[:, t % 2]).then_inc(x1_stored[t % 2], 16)

            def body(g, par):
                if not isinstance(g, int) or g + 3 < NG:
                    load_x(g + 3, 1 - par)
                if "U" in kinds_of(g):
                    load_mask(g + 1, 1 - par)
                load_xres(g, 0)
                load_xres(g, 1)
                store_x1(g, 0)
                load_xres(g, 2)
                store_x1(g, 1)
                load_xres(g, 3)
                store_x1(g, 2)
                store_x1(g, 3)

            load_x(0, 0)
            for i, w in enumerate((wq, wk, wv)):
                sp.dma_start(raw[i], w.rearrange("(c p) n -> p c n", p=P)).then_inc(w_loaded[i], 16)
            load_x(1, 1)
            load_mask(0, 0)
            sp.wait_ge(w_lo_done, 1)
            sp.dma_start(raw[3], wo.rearrange("(c p) n -> p c n", p=P)).then_inc(w_loaded[3], 16)
            load_x(2, 0)
            body(0, 0)
            with sp.Fori(1, NG - 4, 2) as g:
                body(g, 1)
                body(g + 1, 0)
            for g in range(NG - 3, NG):
                body(g, g % 2)
            for i in range(2):
                sp.wait_ge(x1_stored[i], 16 * 2 * NG)

        @block.gpsimd
        def _(pool):
            pool.memset(ident[:, :], 0.0).then_inc(filled, 1)
            pool.memset(minus_half[:, :], -0.5).then_inc(filled, 1)
            pool.wait_ge(filled, 2)
            pool.affine_select(out=ident[:, :], in_=ident[:, :], compare_op=ALU.not_equal, fill=1.0,
                               base=0, pattern=[[-1, P]], channel_multiplier=1).then_inc(ident_done, 1)

            def rstd_of(g):
                pool.wait_ge(var_done, g + 1)
                pool.tensor_tensor(rstd[:, :], var_eps[:, :], minus_half[:, :], ALU.pow).then_inc(rstd_done, 1)

            def fill_neg(g, t):
                wait_apart(pool, exp_done, TILES * g + t - 1, fill_passed)
                pool.memset(scores[:, t % 2], NEG).then_inc(neg_filled, 1)

            def bias_xres(g, t):
                pool.wait_ge(xres_loaded[t % 2], 16 * (2 * g + t // 2 + 1))
                pool.tensor_tensor(xres[:, t % 2], xres[:, t % 2], bo_all[:, :], ALU.add).then_inc(xres_biased, 1)

            def body(g):
                fill_neg(g, 0)
                fill_neg(g, 1)
                bias_xres(g, 0)
                bias_xres(g, 1)
                fill_neg(g, 2)
                if "T" in kinds_of(g):
                    rstd_of(g + 2)
                fill_neg(g, 3)
                bias_xres(g, 2)
                bias_xres(g, 3)

            rstd_of(0)
            for par in range(2):
                pool.memset(kT[par][:, :, :, :], 0.0).then_inc(zeroed, 1)
                pool.memset(prob[:, par], 0.0).then_inc(zeroed, 1)
            rstd_of(1)
            pool.wait_ge(consts_loaded, 16 * 6)
            body(0)
            with pool.Fori(1, NG - 4, 2) as g:
                body(g)
                body(g + 1)
            for g in range(NG - 3, NG):
                body(g)

        @block.scalar
        def _(act):
            with nc.allow_non_contiguous_dma(reason="512 values, one per channel"):
                for i, b in enumerate((ln_g, ln_b, bq, bk)):
                    act.dma_start(cols[:, i], b.rearrange("(c p) -> p c", p=P)).then_inc(consts_loaded, 16)
            act.dma_start(bv_all[:, :], bv.partition_broadcast(P)).then_inc(consts_loaded, 16)
            act.dma_start(bo_all[:, :], bo.partition_broadcast(P)).then_inc(consts_loaded, 16)

            def weight_hi(i):
                act.wait_ge(w_loaded[i], 16)
                act.activation(w_hi[i][:, :, :], raw[i], ACT.Copy).then_inc(w_hi_done, 1)

            def affine(g, k, bank):
                act.wait_ge(t_done, KC * g + k + 1)
                wait(act, nx_split, KC * g + k - 1)
                act.activation(nxT[:, k % 2], lin[bank][:, :], ACT.Identity, scale=cols[:, 0, k:k + 1],
                               bias=cols[:, 1, k:k + 1]).then_inc(nx_done, 1)

            def take_q(g, par, m, bank):
                act.wait_ge(u_done, UNITS * g + 3 * m + 1)
                act.activation(qT[par][:, m, :], lin[bank][:, :], ACT.Identity,
                               bias=cols[:, 2, m:m + 1]).then_inc(q_done, 1)

            def take_k(g, par, m, bank):
                act.wait_ge(u_done, UNITS * g + 3 * m + 2)
                for h in range(2):
                    rows = slice(h * HD, (h + 1) * HD)
                    act.activation(kT[par][rows, :, m, h * P:(h + 1) * P],
                                   lin[bank][rows, :].rearrange("p (t n) -> p t n", n=P), ACT.Identity,
                                   bias=cols[rows, 3, m:m + 1]).then_inc(k_done, 1)

            def exponent(g, t):
                act.wait_ge(shifted, TILES * g + t + 1)
                wait(act, prob_done, TILES * g + t - 1)
                act.activation(expd[:, t % 2], scores[:, t % 2], ACT.Exp, scale=SCALE).then_inc(exp_done, 1)

            def take_probT(g, t):
                act.wait_ge(pt_done, TILES * g + t + 1)
                wait(act, o_done, TILES * g + t - 1)
                act.activation(probT[:, t % 2], ps_probT[:, :], ACT.Copy).then_inc(probT_done, 1)

            def att_hi(g, t):
                act.wait_ge(o_done, TILES * g + t + 1)
                wait(act, proj_done, TILES * g + t - 1)
                act.activation(attT_hi[:, t % 2], lin[bank_of(g, "O", t)][:, :], ACT.Copy)\
                   .then_inc(att_hi_done, 1)

            def body(g, par):
                def unit(j):
                    if "U" in kinds_of(g):
                        take = take_q if j % 3 == 0 else take_k
                        take(g + 1, 1 - par, j // 3, bank_of(g, "U", j))
                unit(0)
                exponent(g, 0)
                unit(1)
                exponent(g, 1)
                take_probT(g, 0)
                unit(3)
                exponent(g, 2)
                att_hi(g, 0)
                unit(4)
                take_probT(g, 1)
                exponent(g, 3)
                unit(6)
                att_hi(g, 1)
                take_probT(g, 2)
                unit(7)
                att_hi(g, 2)
                take_probT(g, 3)
                unit(9)
                unit(10)
                att_hi(g, 3)
                if "T" in kinds_of(g):
                    for k in range(KC):
                        affine(g + 2, k, bank_of(g, "T", k))

            act.wait_ge(consts_loaded, 16 * 6)
            for i in range(3):
                weight_hi(i)
            for k in range(KC):
                affine(0, k, bank_of(-2, "T", k))
            act.wait_ge(zeroed, 2)
            for m in range(KC):
                take_q(0, 0, m, bank_of(-1, "U", 3 * m))
                take_k(0, 0, m, bank_of(-1, "U", 3 * m + 1))
            weight_hi(3)
            for k in range(KC):
                affine(1, k, bank_of(-1, "T", k))
            act.wait_ge(w_lo_done, 4)
            act.wait_ge(zeroed, 4)
            body(0, 0)
            with act.Fori(1, NG - 4, 2) as g:
                body(g, 1)
                body(g + 1, 0)
            for g in range(NG - 3, NG):
                body(g, g % 2)

        @block.vector
        def _(dve):
            def weight_lo(i):
                dve.wait_ge(w_hi_done, i + 1)
                dve.tensor_tensor(w_lo[i][:, :, :], raw[i], w_hi[i][:, :, :].bitcast(F32),
                                  ALU.subtract).then_inc(w_lo_done, 1)

            def ln_stats(g, par, t):
                if t == 0:
                    dve.wait_ge(x_loaded[par], 8 * (g - par) + 16)
                dve.bn_stats(stats[:, t, :], x[par][:, t, :]).then_inc(stats_done, 1)

            def ln_var(g):
                wait_apart(dve, stats_done, TILES * (g + 1), stats_passed)
                for t in range(TILES):
                    dve.bn_aggr(moments[:, t, :], stats[:, t, :]).then_inc(moments_done, 1)
                dve.wait_ge(moments_done, TILES * (g + 1))
                dve.tensor_scalar(var_eps[:, :], moments[:, :, 1], EPS, None, ALU.add).then_inc(var_done, 1)

            def ln_norm(g, par, t):
                dve.wait_ge(rstd_done, g + 1)
                dve.tensor_scalar(x[par][:, t, :], x[par][:, t, :], moments[:, t, 0:1], rstd[:, t:t + 1],
                                  ALU.subtract, ALU.mult).then_inc(zn_done, 1)

            def split_nx(g, k):
                dve.wait_ge(nx_done, KC * g + k + 1)
                wait(dve, u_done, UNITS * g)
                dve.tensor_copy(nxT_hi[:, k], nxT[:, k % 2]).then_inc(nx_hi_done, 1)
                dve.wait_ge(nx_hi_done, KC * g + k + 1)
                dve.tensor_tensor(nxT_lo[:, k], nxT[:, k % 2], nxT_hi[:, k].bitcast(F32),
                                  ALU.subtract).then_inc(nx_split, 1)

            def take_v(g, par, t, bank):
                dve.wait_ge(u_done, UNITS * g + 3 * t + 3)
                dve.tensor_tensor(v[par][:, t, :], lin[bank][:, :], bv_all[:, :], ALU.add).then_inc(v_done, 1)

            def mask_and_shift(g, par, t):
                n = TILES * g + t
                if t == 0:
                    dve.wait_ge(mask_loaded[par], 8 * (g - par) + 16)
                dve.wait_ge(neg_filled, n + 1)
                wait_apart(dve, s_done, n + 1, mask_passed)
                for a in range(2):
                    rows = slice(a * NODES, (a + 1) * NODES)
                    flags = mask[rows, par, t, :].unsqueeze(1).broadcast_to((NODES, HEADS, NODES))
                    ins = dve.copy_predicated(scores[rows, t % 2], flags,
                                              ps_scores[rows, :, a * NODES:(a + 1) * NODES])
                ins.then_inc(masked, 1)
                dve.wait_ge(masked, n + 1)
                dve.tensor_reduce(row_max[:, :], scores[:, t % 2], AX.X, ALU.max).then_inc(max_done, 1)
                dve.wait_ge(max_done, n + 1)
                dve.tensor_tensor(scores[:, t % 2], scores[:, t % 2],
                                  row_max[:, :].unsqueeze(2).broadcast_to((P, HEADS, NODES)),
                                  ALU.subtract).then_inc(shifted, 1)

            def normalise(g, t):
                n = TILES * g + t
                dve.wait_ge(exp_done, n + 1)
                dve.tensor_reduce(row_sum[:, :], expd[:, t % 2], AX.X, ALU.add).then_inc(sum_done, 1)
                dve.wait_ge(sum_done, n + 1)
                dve.reciprocal(row_inv[:, :], row_sum[:, :]).then_inc(inv_done, 1)
                dve.wait_ge(inv_done, n + 1)
                wait(dve, pt_done, n - 1)
                for a in range(2):
                    rows = slice(a * NODES, (a + 1) * NODES)
                    ins = dve.tensor_tensor(prob[rows, t % 2, :, a * NODES:(a + 1) * NODES], expd[rows, t % 2],
                                            row_inv[rows, :].unsqueeze(2).broadcast_to((NODES, HEADS, NODES)),
                                            ALU.mult)
                ins.then_inc(prob_done, 1)

            def att_lo(g, t):
                bank = bank_of(g, "O", t)
                n = TILES * g + t
                dve.wait_ge(att_hi_done, n + 1)
                dve.tensor_tensor(attT_lo[:, t % 2], lin[bank][:, :], attT_hi[:, t % 2].bitcast(F32),
                                  ALU.subtract).then_inc(att_split, 1)

            def residual(g, t):
                bank = bank_of(g, "W", t)
                n = TILES * g + t
                dve.wait_ge(proj_done, n + 1)
                dve.wait_ge(xres_biased, n + 1)
                dve.tensor_tensor(xres[:, t % 2], lin[bank][:, :], xres[:, t % 2], ALU.add).then_inc(x1_done, 1)

            def body(g, par):
                def unit_v(t):
                    if "U" in kinds_of(g):
                        take_v(g + 1, 1 - par, t, bank_of(g, "U", 3 * t + 2))
                ln = "T" in kinds_of(g)
                mask_and_shift(g, par, 0)
                if ln:
                    ln_stats(g + 2, par, 0)
                    ln_stats(g + 2, par, 1)
                normalise(g, 0)
                mask_and_shift(g, par, 1)
                unit_v(0)
                if ln:
                    ln_stats(g + 2, par, 2)
                    ln_stats(g + 2, par, 3)
                    ln_var(g + 2)
                normalise(g, 1)
                mask_and_shift(g, par, 2)
                att_lo(g, 0)
                if ln:
                    ln_norm(g + 2, par, 0)
                    ln_norm(g + 2, par, 1)
                unit_v(1)
                normalise(g, 2)
                mask_and_shift(g, par, 3)
                residual(g, 0)
                if ln:
                    ln_norm(g + 2, par, 2)
                    ln_norm(g + 2, par, 3)
                att_lo(g, 1)
                normalise(g, 3)
                residual(g, 1)
                att_lo(g, 2)
                unit_v(2)
                residual(g, 2)
                att_lo(g, 3)
                unit_v(3)
                if ln:
                    for k in range(KC):
                        split_nx(g + 2, k)
                residual(g, 3)

            for g in range(2):
                for t in range(TILES):
                    ln_stats(g, g, t)
                ln_var(g)
                for t in range(TILES):
                    ln_norm(g, g, t)
                if g == 0:
                    for i in range(3):
                        weight_lo(i)
                    for k in range(KC):
                        split_nx(0, k)
            dve.wait_ge(consts_loaded, 16 * 6)
            for t in range(TILES):
                take_v(0, 0, t, bank_of(-1, "U", 3 * t + 2))
            weight_lo(3)
            for k in range(KC):
                split_nx(1, k)
            body(0, 0)
            with dve.Fori(1, NG - 4, 2) as g:
                body(g, 1)
                body(g + 1, 0)
            for g in range(NG - 3, NG):
                body(g, g % 2)

        @block.tensor
        def _(pe):
            def take_bank(g, kind, n):
                bank, last = ring_place(g, kind, n)
                if last is not None:
                    i, kind, n = last
                    which = {"U": (q_done, k_done, v_done)[n % 3], "T": nx_done, "O": att_split, "W": x1_done}[kind]
                    if kind == "U":
                        per = 2 if n % 3 == 1 else 1
                        pe.wait_ge(which, per * (KC * (i + 1) + n // 3 + 1))
                    elif kind == "T":
                        pe.wait_ge(which, KC * (i + 2) + n + 1)
                    else:
                        pe.wait_ge(which, TILES * i + n + 1)
                return lin[bank]

            def transposes(g, par, k, bank):
                pe.wait_ge(zn_done, TILES * (g + 1))
                for t in range(TILES):
                    mm = pe.transpose(bank[:, t * P:(t + 1) * P], x[par][:, t, k * P:(k + 1) * P], ident[:, :])
                mm.then_inc(t_done, 1)

            def unit(g, j, bank):
                m, which = j // 3, j % 3
                for c in range(KC):
                    if j == 0:
                        pe.wait_ge(nx_split, KC * g + c + 1)
                    nx = (nxT_hi[:, c, :], nxT_lo[:, c, :])
                    if which < 2:
                        lhs = tuple(w[which][:, c, m * P:(m + 1) * P] for w in (w_hi, w_lo))
                        rhs = nx
                    else:
                        lhs = tuple(n[:, m * P:(m + 1) * P] for n in nx)
                        rhs = tuple(w[2][:, c, :] for w in (w_hi, w_lo))
                    mm = split3(pe, bank[:, :], lhs, rhs, c == 0, c == KC - 1)
                mm.then_inc(u_done, 1)

            def score(g, par, t):
                n = TILES * g + t
                if t == 0:
                    pe.wait_ge(q_done, KC * (g + 1))
                    pe.wait_ge(k_done, 2 * KC * (g + 1))
                wait(pe, masked, n)
                for m in range(KC):
                    mm = pe.matmul(ps_scores[:, 2 * m:2 * m + 2, :].rearrange("p h n -> p (h n)"),
                                   qT[par][:, m, t * P:(t + 1) * P], kT[par][:, t, m, :], start=True, stop=True)
                mm.then_inc(s_done, 1)

            def prob_transposes(g, t):
                n = TILES * g + t
                pe.wait_ge(prob_done, n + 1)
                wait(pe, probT_done, n)
                for h in range(HEADS):
                    mm = pe.transpose(ps_probT[:, h * P:(h + 1) * P], prob[:, t % 2, h, :], ident[:, :])
                mm.then_inc(pt_done, 1)

            def attend(g, par, t, bank):
                pe.wait_ge(probT_done, TILES * g + t + 1)
                if t == 0:
                    pe.wait_ge(v_done, TILES * (g + 1))
                for h in range(HEADS):
                    rows = slice((h % 2) * HD, (h % 2 + 1) * HD)
                    mm = pe.matmul(bank[rows, (h // 2) * P:(h // 2 + 1) * P], v[par][:, t, h * HD:(h + 1) * HD],
                                   probT[:, t % 2, h * P:(h + 1) * P], start=True, stop=True)
                mm.then_inc(o_done, 1)

            def project(g, t, bank):
                pe.wait_ge(att_split, TILES * g + t + 1)
                for c in range(KC):
                    mm = split3(pe, bank[:, :], tuple(a[:, t % 2, c * P:(c + 1) * P] for a in (attT_hi, attT_lo)),
                                tuple(w[3][:, c, :] for w in (w_hi, w_lo)), c == 0, c == KC - 1)
                mm.then_inc(proj_done, 1)

            def body(g, par):
                for kind, n in order_of(g):
                    if kind == "S":
                        score(g, par, n)
                    elif kind == "P":
                        prob_transposes(g, n)
                    elif kind == "U":
                        unit(g + 1, n, take_bank(g, "U", n))
                    elif kind == "O":
                        attend(g, par, n, take_bank(g, "O", n))
                    elif kind == "W":
                        project(g, n, take_bank(g, "W", n))
                    else:
                        transposes(g + 2, par, n, take_bank(g, "T", n))

            pe.wait_ge(ident_done, 1)
            body(-2, 0)
            pe.wait_ge(w_lo_done, 3)
            body(-1, 1)
            body(0, 0)
            with pe.Fori(1, NG - 4, 2) as g:
                body(g, 1)
                body(g + 1, 0)
            for g in range(NG - 3, NG):
                body(g, g % 2)


WCH = 8
PIECES = [(1, 0)] + [p for c in range(1, WCH) for p in ((1, c), (2, c - 1))] + [(2, WCH - 1)]
RAW = 3
HR = 4
LAG = 2


def mlp_phase(nc, ins, x1_dram, out_dram):
    ln_g, ln_b, w1, b1, w2, b2 = ins
    x1_groups = x1_dram.rearrange("(g t p) n -> g p t n", t=TILES, p=P)
    out_tiles = out_dram.rearrange("(n p) d -> n p d", p=P)
    w1_cols = w1.rearrange("(c p) n -> p c n", p=P)
    w2_rows = w2.rearrange("(c p) n -> p c n", p=P)
    W1C, W2C = FF // WCH, FC // WCH

    with ExitStack() as ctx:
        def sb(name, shape, dt=F32):
            return ctx.enter_context(nc.sbuf_tensor(name, shape, dt))

        def sem(name):
            return ctx.enter_context(nc.semaphore(name))

        w1_hi, w1_lo = (sb(f"w1_{s}", [P, KC, FF], F32R) for s in ("hi", "lo"))
        w2_hi, w2_lo = (sb(f"w2_{s}", [P, FC, HID], F32R) for s in ("hi", "lo"))
        raw = sb("raw", [P, RAW, KC * W1C])
        x1 = [sb(f"x1_{i}", [P, TILES, HID]) for i in range(2)]
        zn = sb("zn", [P, TILES, HID])
        nxT = sb("mlp_nxT", [P, 2, GT])
        nxT_hi = sb("mlp_nxT_hi", [P, KC, GT], F32R)
        nxT_lo = sb("mlp_nxT_lo", [P, KC, GT], F32R)
        hT = sb("hT", [P, 2, GT])
        hT_hi = sb("hT_hi", [P, HR, GT], F32R)
        hT_lo = sb("hT_lo", [P, HR, GT], F32R)
        b2_all = sb("b2_all", [P, HID])
        ident = sb("mlp_ident", [P, P])
        cols = sb("mlp_cols", [P, 2, KC])
        b1_cols = sb("b1_cols", [P, FC])
        stats = sb("mlp_stats", [P, TILES, 6])
        moments = sb("mlp_moments", [P, TILES, 2])
        var_eps = sb("mlp_var_eps", [P, TILES])
        rstd = sb("mlp_rstd", [P, TILES])
        minus_half = sb("mlp_minus_half", [P, TILES])

        ps_out = [ctx.enter_context(nc.psum_tensor(f"ps_out{i}", [P, HID], F32)) for i in range(TILES)]
        ps_h = [ctx.enter_context(nc.psum_tensor(f"ps_h{i}", [P, GT], F32)) for i in range(2)]
        ps_t = [ctx.enter_context(nc.psum_tensor(f"ps_t{i}", [P, GT], F32)) for i in range(2)]

        x1_loaded = [sem(f"x1_loaded{i}") for i in range(2)]
        out_stored = [sem(f"out_stored{i}") for i in range(2)]
        raw_loaded = [sem(f"raw_loaded{i}") for i in range(RAW)]
        consts_loaded = sem("mlp_consts_loaded")
        piece_hi, piece_lo = sem("piece_hi"), sem("piece_lo")
        filled, ident_done = sem("mlp_filled"), sem("mlp_ident_done")
        stats_done, moments_done, var_done = sem("mlp_stats_done"), sem("mlp_moments_done"), sem("mlp_var_done")
        rstd_done, zn_done, t_done = sem("mlp_rstd_done"), sem("mlp_zn_done"), sem("mlp_t_done")
        nx_done, nx_hi_done, nx_split = sem("mlp_nx_done"), sem("mlp_nx_hi_done"), sem("mlp_nx_split")
        stats_passed = sem("mlp_stats_passed")
        up_done, gelu_done, h_hi_done = sem("up_done"), sem("gelu_done"), sem("h_hi_done")
        h_split, down_done = sem("h_split"), sem("down_done")
        x1_biased, out_done = sem("x1_biased"), sem("out_done")

        def piece_views(n):
            which, c = PIECES[n]
            if which == 1:
                cut = slice(c * W1C, (c + 1) * W1C)
                return (raw[:, n % RAW, :].rearrange("p (c n) -> p c n", c=KC), w1_cols[:, :, cut],
                        w1_hi[:, :, cut], w1_lo[:, :, cut])
            cut = slice(c * W2C, (c + 1) * W2C)
            return (raw[:, n % RAW, :].rearrange("p (c n) -> p c n", c=W2C), w2_rows[:, cut, :],
                    w2_hi[:, cut, :], w2_lo[:, cut, :])

        block = ctx.enter_context(nc.Block())

        @block.sync
        def _(sp):
            def load_piece(n):
                wait(sp, piece_lo, n - RAW + 1)
                to, source, _, _ = piece_views(n)
                sp.dma_start(to, source).then_inc(raw_loaded[n % RAW], 16)

            def load_x1(g, par):
                wait(sp, out_stored[par], 32 * (g - par) if not isinstance(g, int) else 64 * (g // 2))
                sp.dma_start(x1[par][:, :, :], x1_groups[g]).then_inc(x1_loaded[par], 16)

            def body(g, par):
                if not isinstance(g, int) or g + 1 < NG:
                    load_x1(g + 1, 1 - par)
                if isinstance(g, int) and g == 0:
                    for n in range(RAW, len(PIECES)):
                        load_piece(n)
                for t in range(TILES):
                    sp.wait_ge(out_done, TILES * g + t + 1)
                    sp.dma_start(out_tiles[g * TILES + t], x1[par][:, t, :]).then_inc(out_stored[par], 16)

            load_x1(0, 0)
            for n in range(RAW):
                load_piece(n)
            body(0, 0)
            with sp.Fori(1, NG - 2, 2) as g:
                body(g, 1)
                body(g + 1, 0)
            body(NG - 1, 1)
            for i in range(2):
                sp.wait_ge(out_stored[i], 16 * TILES * NG // 2)

        @block.gpsimd
        def _(pool):
            pool.memset(ident[:, :], 0.0).then_inc(filled, 1)
            pool.memset(minus_half[:, :], -0.5).then_inc(filled, 1)
            pool.wait_ge(filled, 2)
            pool.affine_select(out=ident[:, :], in_=ident[:, :], compare_op=ALU.not_equal, fill=1.0,
                               base=0, pattern=[[-1, P]], channel_multiplier=1).then_inc(ident_done, 1)

            def ln(g, par):
                pool.wait_ge(var_done, g + 1)
                pool.tensor_tensor(rstd[:, :], var_eps[:, :], minus_half[:, :], ALU.pow).then_inc(rstd_done, 1)
                for t in range(TILES):
                    pool.wait_ge(zn_done, TILES * g + t + 1)
                    pool.tensor_tensor(x1[par][:, t, :], x1[par][:, t, :], b2_all[:, :], ALU.add)\
                        .then_inc(x1_biased, 1)

            pool.wait_ge(consts_loaded, 16 * 4)
            ln(0, 0)
            ln(1, 1)
            with pool.Fori(1, NG - 2, 2) as g:
                ln(g + 1, 0)
                ln(g + 2, 1)

        @block.scalar
        def _(act):
            with nc.allow_non_contiguous_dma(reason="one value per channel"):
                for i, b in enumerate((ln_g, ln_b)):
                    act.dma_start(cols[:, i], b.rearrange("(c p) -> p c", p=P)).then_inc(consts_loaded, 16)
                act.dma_start(b1_cols[:, :], b1.rearrange("(c p) -> p c", p=P)).then_inc(consts_loaded, 16)
            act.dma_start(b2_all[:, :], b2.partition_broadcast(P)).then_inc(consts_loaded, 16)

            def split_hi(n):
                act.wait_ge(raw_loaded[n % RAW], 16 * (n // RAW + 1))
                source, _, hi, _ = piece_views(n)
                act.activation(hi, source, ACT.Copy).then_inc(piece_hi, 1)

            def affine(g, k):
                act.wait_ge(t_done, KC * g + k + 1)
                wait(act, nx_split, KC * g + k - 1)
                act.activation(nxT[:, k % 2], ps_t[k % 2][:, :], ACT.Identity, scale=cols[:, 0, k:k + 1],
                               bias=cols[:, 1, k:k + 1]).then_inc(nx_done, 1)

            def body(g):
                for m in range(FC):
                    n = FC * g + m
                    act.wait_ge(up_done, n + 1)
                    wait(act, h_split, n - 1)
                    act.activation(hT[:, m % 2], ps_h[m % 2][:, :], ACT.Gelu,
                                   bias=b1_cols[:, m:m + 1]).then_inc(gelu_done, 1)
                    act.wait_ge(gelu_done, n + 1)
                    wait(act, down_done, n - HR + 1)
                    act.activation(hT_hi[:, m % HR], hT[:, m % 2], ACT.Copy).then_inc(h_hi_done, 1)
                    if isinstance(g, int) and g == 0 and m + 2 < len(PIECES):
                        split_hi(m + 2)
                if not isinstance(g, int) or g + 1 < NG:
                    for k in range(KC):
                        affine(g + 1, k)

            act.wait_ge(consts_loaded, 16 * 4)
            split_hi(0)
            split_hi(1)
            for k in range(KC):
                affine(0, k)
            body(0)
            with act.Fori(1, NG - 2, 2) as g:
                body(g)
                body(g + 1)
            body(NG - 1)

        @block.vector
        def _(dve):
            def split_lo(n):
                dve.wait_ge(piece_hi, n + 1)
                source, _, hi, lo = piece_views(n)
                dve.tensor_tensor(lo, source, hi.bitcast(F32), ALU.subtract).then_inc(piece_lo, 1)

            def ln_stats(g, par, t):
                if t == 0:
                    dve.wait_ge(x1_loaded[par], 8 * (g - par) + 16)
                dve.bn_stats(stats[:, t, :], x1[par][:, t, :]).then_inc(stats_done, 1)

            def ln_var(g):
                wait_apart(dve, stats_done, TILES * (g + 1), stats_passed)
                for t in range(TILES):
                    dve.bn_aggr(moments[:, t, :], stats[:, t, :]).then_inc(moments_done, 1)
                dve.wait_ge(moments_done, TILES * (g + 1))
                dve.tensor_scalar(var_eps[:, :], moments[:, :, 1], EPS, None, ALU.add).then_inc(var_done, 1)

            def ln_norm(g, par, t):
                dve.wait_ge(rstd_done, g + 1)
                wait(dve, t_done, KC * g)
                dve.tensor_scalar(zn[:, t, :], x1[par][:, t, :], moments[:, t, 0:1], rstd[:, t:t + 1],
                                  ALU.subtract, ALU.mult).then_inc(zn_done, 1)

            def split_nx(g, k):
                dve.wait_ge(nx_done, KC * g + k + 1)
                wait(dve, up_done, FC * g)
                dve.tensor_copy(nxT_hi[:, k], nxT[:, k % 2]).then_inc(nx_hi_done, 1)
                dve.wait_ge(nx_hi_done, KC * g + k + 1)
                dve.tensor_tensor(nxT_lo[:, k], nxT[:, k % 2], nxT_hi[:, k].bitcast(F32),
                                  ALU.subtract).then_inc(nx_split, 1)

            def body(g, par):
                more = not isinstance(g, int) or g + 1 < NG
                for m in range(FC):
                    dve.wait_ge(h_hi_done, FC * g + m + 1)
                    dve.tensor_tensor(hT_lo[:, m % HR], hT[:, m % 2], hT_hi[:, m % HR].bitcast(F32),
                                      ALU.subtract).then_inc(h_split, 1)
                    if isinstance(g, int) and g == 0 and m + 2 < len(PIECES):
                        split_lo(m + 2)
                    if more and 3 <= m < 3 + TILES:
                        ln_stats(g + 1, 1 - par, m - 3)
                    if more and m == 3 + TILES:
                        ln_var(g + 1)
                    if more and 9 <= m < 9 + TILES:
                        ln_norm(g + 1, 1 - par, m - 9)
                if more:
                    for k in range(KC):
                        split_nx(g + 1, k)
                dve.wait_ge(down_done, FC * (g + 1))
                for t in range(TILES):
                    dve.wait_ge(x1_biased, TILES * g + t + 1)
                    dve.tensor_tensor(x1[par][:, t, :], ps_out[t][:, :], x1[par][:, t, :], ALU.add)\
                       .then_inc(out_done, 1)

            for t in range(TILES):
                ln_stats(0, 0, t)
            ln_var(0)
            for t in range(TILES):
                ln_norm(0, 0, t)
            split_lo(0)
            split_lo(1)
            for k in range(KC):
                split_nx(0, k)
            body(0, 0)
            with dve.Fori(1, NG - 2, 2) as g:
                body(g, 1)
                body(g + 1, 0)
            body(NG - 1, 1)

        @block.tensor
        def _(pe):
            def transposes(g):
                pe.wait_ge(zn_done, TILES * (g + 1))
                for k in range(KC):
                    wait(pe, nx_done, KC * g + k - 1)
                    for t in range(TILES):
                        mm = pe.transpose(ps_t[k % 2][:, t * P:(t + 1) * P], zn[:, t, k * P:(k + 1) * P],
                                          ident[:, :])
                    mm.then_inc(t_done, 1)

            def up(g, m):
                n = FC * g + m
                wait(pe, gelu_done, n - 1)
                if isinstance(g, int) and g == 0 and m % 2 == 0:
                    pe.wait_ge(piece_lo, PIECES.index((1, m // 2)) + 1)
                for c in range(KC):
                    if m == 0:
                        pe.wait_ge(nx_split, KC * g + c + 1)
                    mm = split3(pe, ps_h[m % 2][:, :], tuple(w[:, c, m * P:(m + 1) * P] for w in (w1_hi, w1_lo)),
                                (nxT_hi[:, c, :], nxT_lo[:, c, :]), c == 0, c == KC - 1)
                mm.then_inc(up_done, 1)

            def down(g, m):
                pe.wait_ge(h_split, FC * g + m + 1)
                if m == 0:
                    wait(pe, out_done, TILES * g)
                if isinstance(g, int) and g == 0 and m % 2 == 0:
                    pe.wait_ge(piece_lo, PIECES.index((2, m // 2)) + 1)
                for t in range(TILES):
                    mm = split3(pe, ps_out[t][:, :], tuple(h[:, m % HR, t * P:(t + 1) * P] for h in (hT_hi, hT_lo)),
                                (w2_hi[:, m, :], w2_lo[:, m, :]), m == 0, m == FC - 1)
                mm.then_inc(down_done, 1)

            def body(g):
                for m in range(FC):
                    up(g, m)
                    if m >= LAG:
                        down(g, m - LAG)
                if not isinstance(g, int) or g + 1 < NG:
                    transposes(g + 1)
                for m in range(FC - LAG, FC):
                    down(g, m)

            pe.wait_ge(ident_done, 1)
            transposes(0)
            body(0)
            with pe.Fori(1, NG - 2, 2) as g:
                body(g)
                body(g + 1)
            body(NG - 1)


def adj_layer(nc, x, adj, ln1_g, ln1_b, ln2_g, ln2_b, wq, bq, wk, bk, wv, bv, wo, bo, w1, b1, w2, b2, out):
    x1 = nc.dram_tensor("x1_scratch", (TOKENS, HID), F32, kind="Internal").ap()
    attention_phase(nc, (x, adj, ln1_g, ln1_b, wq, bq, wk, bk, wv, bv, wo, bo), x1)
    mlp_phase(nc, (ln2_g, ln2_b, w1, b1, w2, b2), x1, out)


_INS = ["x", "adj"] + [f"L0_gnn_{n}" for n in ("ln1_g", "ln1_b", "ln2_g", "ln2_b", "Wq", "bq", "Wk", "bk", "Wv", "bv",
                                               "Wo", "bo", "W1", "b1", "W2", "b2")]


def kernel(**inputs):
    import numpy as np
    import concourse.bacc as bacc
    from concourse.bass_utils import run_bass_kernel_spmd

    nc = bacc.Bacc("TRN2", target_bir_lowering=False, num_devices=1)
    arrays, args = {}, []
    for name in _INS:
        a = np.ascontiguousarray(inputs[name])
        if name == "x":
            a = a.reshape(TOKENS, HID)
        arrays[f"in_{name}"] = a
        args.append(nc.dram_tensor(f"in_{name}", a.shape, mybir.dt.from_np(a.dtype), kind="ExternalInput").ap())
    out = nc.dram_tensor("out", (TOKENS, HID), F32, kind="ExternalOutput").ap()
    adj_layer(nc, *args, out)
    r = run_bass_kernel_spmd(nc, [arrays], core_ids=[0])
    return r.results[0]["out"].reshape(GRAPHS, NODES, HID)
```

```python
from contextlib import ExitStack

import concourse.bass as bass
from concourse import mybir

F32 = mybir.dt.float32
F32R = mybir.dt.float32r
U8 = mybir.dt.uint8
ALU = mybir.AluOpType
ACT = mybir.ActivationFunctionType
AX = mybir.AxisListType

P = 128
GRAPHS, NODES, HID = 128, 64, 512
HEADS = 8
HD = HID // HEADS
FF = 4 * HID
TOKENS = GRAPHS * NODES
KC = HID // P
FC = FF // P
TILES = 4
GT = TILES * P
NG = TOKENS // GT
EPS = 1e-5
SCALE = HD ** -0.5
NEG = -1.0e9 / SCALE

UNITS = 3 * KC
ORDER = [("S", 0), ("U", 0), ("U", 1), ("S", 1), ("U", 2), ("P", 0), ("U", 3), ("S", 2), ("O", 0), ("U", 4),
         ("P", 1), ("U", 5), ("S", 3), ("W", 0), ("U", 6), ("O", 1), ("P", 2), ("U", 7), ("W", 1), ("O", 2),
         ("U", 8), ("P", 3), ("U", 9), ("W", 2), ("U", 10), ("O", 3), ("U", 11),
         ("T", 0), ("T", 1), ("T", 2), ("T", 3), ("W", 3)]
LIN = 4


def kinds_of(g):
    if not isinstance(g, int):
        return "SUPOWT"
    return "SPOW" * (g >= 0) + "U" * (0 <= g + 1 < NG) + "T" * (g + 2 < NG)


def order_of(g):
    return [(k, n) for k, n in ORDER if k in kinds_of(g)]


def lin_uses(g):
    return [(g, k, n) for k, n in order_of(g) if k in "UTOW"]


def ring_place(g, kind, n):
    if isinstance(g, int):
        uses = [u for i in range(-2, g + 1) for u in lin_uses(i)]
        at = uses.index((g, kind, n))
        return at % LIN, uses[at - LIN] if at >= LIN else None
    uses = lin_uses(g)
    at = [u[1:] for u in uses].index((kind, n))
    assert len(uses) % LIN == 0 and len(lin_uses(-2) + lin_uses(-1) + lin_uses(0)) % LIN == 0
    return at % LIN, uses[at - LIN] if at >= LIN else (g - 1, *uses[at - LIN][1:])


def bank_of(g, kind, n):
    return ring_place(g, kind, n)[0]


def wait(eng, sem, value):
    if not isinstance(value, int) or value > 0:
        eng.wait_ge(sem, value)


def is_first(g):
    return isinstance(g, int) and g == 0


def is_last(g):
    return isinstance(g, int) and g == NG - 1


def wait_apart(eng, sem, value, passed):
    wait(eng, sem, value)
    if not isinstance(value, int):
        eng.sem_inc(passed, 1)


def split3(pe, out, lhs, rhs, first, last):
    pe.matmul(out, lhs[1], rhs[0], start=first, stop=False)
    pe.matmul(out, lhs[0], rhs[1], start=False, stop=False)
    return pe.matmul(out, lhs[0], rhs[0], start=False, stop=last)


WCH = 8
PIECES = [(1, 0)] + [p for c in range(1, WCH) for p in ((1, c), (2, c - 1))] + [(2, WCH - 1)]
RAW = 3
HR = 4
LAG = 2



def adj_layer(nc, x_dram, adj, ln1_g, ln1_b, ln2_g, ln2_b, wq, bq, wk, bk, wv, bv, wo, bo, w1, b1, w2, b2, out_dram):
    x1_dram = nc.dram_tensor("x1_scratch", (TOKENS, HID), F32, kind="Internal").ap()
    x_groups, x1_groups = (a.rearrange("(g t p) n -> g p t n", t=TILES, p=P) for a in (x_dram, x1_dram))
    x_tiles, x1_tiles, out_tiles = (a.rearrange("(n p) d -> n p d", p=P) for a in (x_dram, x1_dram, out_dram))
    adj_groups = adj.rearrange("(g t a) q k -> g (a q) t k", t=TILES, a=2)
    w1_cols, w2_rows = (a.rearrange("(c p) n -> p c n", p=P) for a in (w1, w2))

    ctx = ExitStack()
    with ctx:
        def placer(stack):
            return lambda name, shape, dt=F32: stack.enter_context(nc.sbuf_tensor(name, shape, dt))

        def sem(name):
            return ctx.enter_context(nc.semaphore(name))

        sb = placer(ctx)
        ident = sb("ident", [P, P])
        minus_half = sb("minus_half", [P, TILES])
        cols = sb("cols", [P, 4, KC])
        mlp_cols = sb("mlp_cols", [P, 2, KC])
        b1_cols = sb("b1_cols", [P, FC])
        stats = sb("stats", [P, TILES, 6])
        moments = sb("moments", [P, TILES, 2])
        var_eps = sb("var_eps", [P, TILES])
        rstd = sb("rstd", [P, TILES])
        row_max = sb("row_max", [P, HEADS])
        row_sum = sb("row_sum", [P, HEADS])
        row_inv = sb("row_inv", [P, HEADS])
        start = nc.sbuf_base

        with ExitStack() as phase:
            sb = placer(phase)
            wqkv_hi, wqkv_lo = ([sb(f"w{c}_{s}", [P, KC, HID], F32R) for c in "qkv"] for s in ("hi", "lo"))
            nxT_hi = sb("nxT_hi", [P, KC, GT], F32R)
            nxT_lo = sb("nxT_lo", [P, KC, GT], F32R)
            nxT = sb("nxT", [P, 2, GT])
            x = [sb(f"x{i}", [P, TILES, HID]) for i in range(2)]
            qT0 = sb("qT0", [P, KC, GT])
            kT0 = sb("kT0", [P, TILES, KC, 2, 2, NODES])
            v0 = sb("v0", [P, TILES, HID])
            early_end = nc.sbuf_base
            wo_hi, wo_lo = (sb(f"wo_{s}", [P, KC, HID], F32R) for s in ("hi", "lo"))
            xres = sb("xres", [P, 2, HID])
            bv_all = sb("bv_all", [P, HID])
            bo_all = sb("bo_all", [P, HID])
            qT = [qT0, sb("qT1", [P, KC, GT])]
            kT = [kT0, sb("kT1", [P, TILES, KC, 2, 2, NODES])]
            v = [v0, sb("v1", [P, TILES, HID])]
            softmax = sb("softmax", [P, 2, 2, HEADS, NODES])
            scores, expd = softmax[:, 0], softmax[:, 1]
            prob = sb("prob", [P, 2, HEADS, NODES])
            probT = sb("probT", [P, 2, KC, 2, 2, NODES])
            attT_hi = sb("attT_hi", [P, 2, HID], F32R)
            attT_lo = sb("attT_lo", [P, 2, HID], F32R)
            mask = sb("mask", [P, 2, TILES, NODES], U8)
            w_hi, w_lo = wqkv_hi + [wo_hi], wqkv_lo + [wo_lo]

        with ExitStack() as phase:
            sb = placer(phase)
            assert nc.sbuf_base == start
            w1_hi, w1_lo = (sb(f"w1_{s}", [P, KC, FF], F32R) for s in ("hi", "lo"))
            mlp_nxT_hi = sb("mlp_nxT_hi", [P, KC, GT], F32R)
            mlp_nxT_lo = sb("mlp_nxT_lo", [P, KC, GT], F32R)
            mlp_nxT = sb("mlp_nxT", [P, 2, GT])
            x1_0 = sb("x1_0", [P, TILES, HID])
            zn = sb("zn", [P, TILES, HID])
            raw = sb("raw", [P, RAW, KC * FF // WCH])
            hT = sb("hT", [P, 2, GT])
            assert nc.sbuf_base <= early_end
            w2_hi, w2_lo = (sb(f"w2_{s}", [P, FC, HID], F32R) for s in ("hi", "lo"))
            x1 = [x1_0, sb("x1_1", [P, TILES, HID])]
            hT_hi = sb("hT_hi", [P, HR, GT], F32R)
            hT_lo = sb("hT_lo", [P, HR, GT], F32R)
            b2_all = sb("b2_all", [P, HID])

        with ExitStack() as phase:
            lin = [phase.enter_context(nc.psum_tensor(f"lin{i}", [P, GT], F32)) for i in range(LIN)]
            ps_scores = phase.enter_context(nc.psum_tensor("ps_scores", [P, 2, HEADS, NODES], F32))
            ps_probT = phase.enter_context(nc.psum_tensor("ps_probT", [P, 2, KC, P], F32))
        with ExitStack() as phase:
            ps_out = [phase.enter_context(nc.psum_tensor(f"ps_out{i}", [P, HID], F32)) for i in range(TILES)]
            ps_t = [phase.enter_context(nc.psum_tensor(f"ps_t{i}", [P, GT], F32)) for i in range(2)]
            ps_h = [phase.enter_context(nc.psum_tensor(f"ps_h{i}", [P, GT], F32)) for i in range(2)]

        raw_w = [qT[1][:, :, :], v[1][:, :, :], softmax.rearrange("p s b h n -> p (s b) (h n)"), qT[1][:, :, :]]

        x0_loaded = [sem(f"x0_loaded{t}") for t in range(TILES)]
        x_loaded = [sem(f"x_loaded{i}") for i in range(2)]
        mask_loaded = [sem(f"mask_loaded{i}") for i in range(2)]
        xres_loaded = [sem(f"xres_loaded{i}") for i in range(2)]
        x1_stored = [sem(f"x1_stored{i}") for i in range(2)]
        w_loaded, w_hi_done, w_lo_done = ([sem(f"w{c}_{s}") for c in "qkvo"] for s in ("loaded", "hi_done", "lo_done"))
        cols_loaded, rows_loaded = sem("cols_loaded"), sem("rows_loaded")
        filled, ident_done, k_zeroed, probT_zeroed = sem("filled"), sem("ident_done"), sem("k_zeroed"), sem("probT_zeroed")
        stats_done, moments_done, var_done = sem("stats_done"), sem("moments_done"), sem("var_done")
        rstd_done, zn_done, t_done = sem("rstd_done"), sem("zn_done"), sem("t_done")
        nx_done, nx_hi_done, nx_split = sem("nx_done"), sem("nx_hi_done"), sem("nx_split")
        u_done, q_done, k_done, v_done = sem("u_done"), sem("q_done"), sem("k_done"), sem("v_done")
        s_done, neg_filled, masked, max_done = sem("s_done"), sem("neg_filled"), sem("masked"), sem("max_done")
        shifted, exp_done, sum_done, inv_done = sem("shifted"), sem("exp_done"), sem("sum_done"), sem("inv_done")
        prob_done, pt_done, probT_done = sem("prob_done"), sem("pt_done"), sem("probT_done")
        o_done, att_hi_done, att_split = sem("o_done"), sem("att_hi_done"), sem("att_split")
        mask_passed, fill_passed, stats_passed = sem("mask_passed"), sem("fill_passed"), sem("stats_passed")
        proj_done, xres_biased, x1_done = sem("proj_done"), sem("xres_biased"), sem("x1_done")
        x1_loaded = [sem(f"x1_loaded{i}") for i in range(2)]
        out_stored = [sem(f"out_stored{i}") for i in range(2)]
        raw_loaded = [sem(f"raw_loaded{i}") for i in range(RAW)]
        b2_loaded = sem("b2_loaded")
        piece_hi, piece_lo = sem("piece_hi"), sem("piece_lo")
        mlp_stats_done, mlp_moments_done, mlp_var_done = (sem(f"mlp_{s}_done") for s in ("stats", "moments", "var"))
        mlp_rstd_done, mlp_zn_done, mlp_t_done = (sem(f"mlp_{s}_done") for s in ("rstd", "zn", "t"))
        mlp_nx_done, mlp_nx_hi_done, mlp_nx_split = sem("mlp_nx_done"), sem("mlp_nx_hi_done"), sem("mlp_nx_split")
        mlp_stats_passed = sem("mlp_stats_passed")
        up_done, gelu_done, h_hi_done = sem("up_done"), sem("gelu_done"), sem("h_hi_done")
        h_split, down_done = sem("h_split"), sem("down_done")
        x1_biased, out_done = sem("x1_biased"), sem("out_done")

        def piece_views(n):
            which, c = PIECES[n]
            per, rows, source, hi, lo = ((FF // WCH, KC, w1_cols, w1_hi, w1_lo) if which == 1 else
                                         (FC // WCH, FC // WCH, w2_rows, w2_hi, w2_lo))
            cut = slice(c * per, (c + 1) * per)
            cut = (slice(None), slice(None), cut) if which == 1 else (slice(None), cut)
            return raw[:, n % RAW, :].rearrange("p (c n) -> p c n", c=rows), source[cut], hi[cut], lo[cut]

        block = ctx.enter_context(nc.Block())

        @block.sync
        def _(sp):
            def load_x(g, par):
                wait(sp, t_done, KC * (g - 1))
                sp.dma_start(x[par][:, :, :], x_groups[g]).then_inc(x_loaded[par], 16)

            def load_mask(g, par):
                with nc.allow_non_contiguous_dma(reason="rows of 64 flags"):
                    sp.dma_start(mask[:, par], adj_groups[g]).then_inc(mask_loaded[par], 16)

            def load_xres(g, t):
                wait(sp, x1_stored[t % 2], 16 * (2 * g + t // 2))
                sp.dma_start(xres[:, t % 2], x_tiles[g * TILES + t]).then_inc(xres_loaded[t % 2], 16)

            def store_x1(g, t):
                sp.wait_ge(x1_done, TILES * g + t + 1)
                sp.dma_start(x1_tiles[g * TILES + t], xres[:, t % 2]).then_inc(x1_stored[t % 2], 16)

            def body(g, par):
                if not isinstance(g, int) or g + 3 < NG:
                    load_x(g + 3, 1 - par)
                if "U" in kinds_of(g):
                    load_mask(g + 1, 1 - par)
                load_xres(g, 0)
                load_xres(g, 1)
                if is_last(g):
                    sp.wait_ge(u_done, UNITS * NG)
                    sp.wait_ge(proj_done, TILES * g)
                    load_x1(0, 0)
                    for n in range(RAW):
                        load_piece(n)
                store_x1(g, 0)
                load_xres(g, 2)
                store_x1(g, 1)
                load_xres(g, 3)
                store_x1(g, 2)
                store_x1(g, 3)

            def load_piece(n):
                wait(sp, piece_lo, n - RAW + 1)
                to, source, _, _ = piece_views(n)
                sp.dma_start(to, source).then_inc(raw_loaded[n % RAW], 16)

            def load_x1(g, par):
                wait(sp, out_stored[par], 32 * (g - par) if not isinstance(g, int) else 64 * (g // 2))
                sp.dma_start(x1[par][:, :, :], x1_groups[g]).then_inc(x1_loaded[par], 16)

            def mlp_body(g, par):
                if not isinstance(g, int) or g + 1 < NG:
                    load_x1(g + 1, 1 - par)
                if is_first(g):
                    for n in range(RAW, len(PIECES)):
                        load_piece(n)
                for t in range(TILES):
                    sp.wait_ge(out_done, TILES * g + t + 1)
                    sp.dma_start(out_tiles[g * TILES + t], x1[par][:, t, :]).then_inc(out_stored[par], 16)

            for t in range(TILES):
                sp.dma_start(x[0][:, t, :], x_tiles[t]).then_inc(x0_loaded[t], 16)
            for i, w in enumerate((wq, wk, wv)):
                sp.dma_start(raw_w[i], w.rearrange("(c p) n -> p c n", p=P)).then_inc(w_loaded[i], 16)
            load_x(1, 1)
            load_mask(0, 0)
            sp.wait_ge(w_lo_done[0], 1)
            sp.dma_start(raw_w[3], wo.rearrange("(c p) n -> p c n", p=P)).then_inc(w_loaded[3], 16)
            load_x(2, 0)
            body(0, 0)
            with sp.Fori(1, NG - 4, 2) as g:
                body(g, 1)
                body(g + 1, 0)
            for g in range(NG - 3, NG):
                body(g, g % 2)
            for i in range(2):
                sp.wait_ge(x1_stored[i], 16 * 2 * NG)
            sp.dma_start(b2_all[:, :], b2.partition_broadcast(P)).then_inc(b2_loaded, 16)
            mlp_body(0, 0)
            with sp.Fori(1, NG - 2, 2) as g:
                mlp_body(g, 1)
                mlp_body(g + 1, 0)
            mlp_body(NG - 1, 1)
            for i in range(2):
                sp.wait_ge(out_stored[i], 16 * TILES * NG // 2)

        @block.gpsimd
        def _(pool):
            pool.memset(ident[:, :], 0.0).then_inc(filled, 1)
            pool.memset(minus_half[:, :], -0.5).then_inc(filled, 1)
            pool.wait_ge(filled, 2)
            pool.affine_select(out=ident[:, :], in_=ident[:, :], compare_op=ALU.not_equal, fill=1.0,
                               base=0, pattern=[[-1, P]], channel_multiplier=1).then_inc(ident_done, 1)

            def rstd_of(g):
                pool.wait_ge(var_done, g + 1)
                pool.tensor_tensor(rstd[:, :], var_eps[:, :], minus_half[:, :], ALU.pow).then_inc(rstd_done, 1)

            def fill_neg(g, t):
                wait_apart(pool, exp_done, TILES * g + t - 1, fill_passed)
                pool.memset(scores[:, t % 2], NEG).then_inc(neg_filled, 1)

            def bias_xres(g, t):
                pool.wait_ge(xres_loaded[t % 2], 16 * (2 * g + t // 2 + 1))
                pool.tensor_tensor(xres[:, t % 2], xres[:, t % 2], bo_all[:, :], ALU.add).then_inc(xres_biased, 1)

            def body(g):
                fill_neg(g, 0)
                fill_neg(g, 1)
                bias_xres(g, 0)
                bias_xres(g, 1)
                fill_neg(g, 2)
                if "T" in kinds_of(g):
                    rstd_of(g + 2)
                fill_neg(g, 3)
                if is_last(g):
                    mlp_rstd(0)
                    split_lo(0)
                    split_lo(1)
                bias_xres(g, 2)
                bias_xres(g, 3)

            def mlp_rstd(g):
                pool.wait_ge(mlp_var_done, g + 1)
                pool.tensor_tensor(rstd[:, :], var_eps[:, :], minus_half[:, :], ALU.pow).then_inc(mlp_rstd_done, 1)

            def bias_x1(g, par, t):
                pool.wait_ge(mlp_zn_done, TILES * g + t + 1)
                pool.tensor_tensor(x1[par][:, t, :], x1[par][:, t, :], b2_all[:, :], ALU.add).then_inc(x1_biased, 1)

            def split_lo(n):
                pool.wait_ge(piece_hi, n + 1)
                source, _, hi, lo = piece_views(n)
                pool.tensor_tensor(lo, source, hi.bitcast(F32), ALU.subtract).then_inc(piece_lo, 1)

            def mlp_ln(g, par):
                mlp_rstd(g)
                for t in range(TILES):
                    bias_x1(g, par, t)

            for par in range(2):
                pool.memset(kT[par][:, :, :, :, :, :], 0.0).then_inc(k_zeroed, 1)
            rstd_of(0)
            pool.wait_ge(w_hi_done[1], 1)
            pool.tensor_tensor(w_lo[1][:, :, :], raw_w[1], w_hi[1][:, :, :].bitcast(F32), ALU.subtract)\
                .then_inc(w_lo_done[1], 1)
            for par in range(2):
                pool.memset(probT[:, par], 0.0).then_inc(probT_zeroed, 1)
            rstd_of(1)
            pool.wait_ge(rows_loaded, 16 * 2)
            pool.wait_ge(w_lo_done[2], 1)
            body(0)
            with pool.Fori(1, NG - 4, 2) as g:
                body(g)
                body(g + 1)
            for g in range(NG - 3, NG):
                body(g)
            pool.wait_ge(b2_loaded, 16)
            for m in range(FC):
                if m + LAG < len(PIECES):
                    split_lo(m + LAG)
                if m < TILES:
                    bias_x1(0, 0, m)
                if m == 7:
                    mlp_rstd(1)
                if 9 <= m < 9 + TILES:
                    bias_x1(1, 1, m - 9)
            with pool.Fori(1, NG - 2, 2) as g:
                mlp_ln(g + 1, 0)
                mlp_ln(g + 2, 1)

        @block.scalar
        def _(act):
            with nc.allow_non_contiguous_dma(reason="one value per channel"):
                for to, b in ((cols[:, 0], ln1_g), (cols[:, 1], ln1_b), (cols[:, 2], bq), (cols[:, 3], bk),
                              (mlp_cols[:, 0], ln2_g), (mlp_cols[:, 1], ln2_b), (b1_cols[:, :], b1)):
                    act.dma_start(to, b.rearrange("(c p) -> p c", p=P)).then_inc(cols_loaded, 16)

            def weight_hi(i):
                act.wait_ge(w_loaded[i], 16)
                act.activation(w_hi[i][:, :, :], raw_w[i], ACT.Copy).then_inc(w_hi_done[i], 1)

            def affine(g, k, bank):
                act.wait_ge(t_done, KC * g + k + 1)
                wait(act, nx_split, KC * g + k - 1)
                act.activation(nxT[:, k % 2], lin[bank][:, :], ACT.Identity, scale=cols[:, 0, k:k + 1],
                               bias=cols[:, 1, k:k + 1]).then_inc(nx_done, 1)

            def take_q(g, par, m, bank):
                act.wait_ge(u_done, UNITS * g + 3 * m + 1)
                act.activation(qT[par][:, m, :], lin[bank][:, :], ACT.Identity,
                               bias=cols[:, 2, m:m + 1]).then_inc(q_done, 1)

            def take_k(g, par, m, bank):
                act.wait_ge(u_done, UNITS * g + 3 * m + 2)
                for h in range(2):
                    rows = slice(h * HD, (h + 1) * HD)
                    act.activation(kT[par][rows, :, m, :, h, :],
                                   lin[bank][rows, :].rearrange("p (t a n) -> p t a n", a=2, n=NODES), ACT.Identity,
                                   bias=cols[rows, 3, m:m + 1]).then_inc(k_done, 1)

            def exponent(g, t):
                act.wait_ge(shifted, TILES * g + t + 1)
                wait(act, prob_done, TILES * g + t - 1)
                act.activation(expd[:, t % 2], scores[:, t % 2], ACT.Exp, scale=SCALE).then_inc(exp_done, 1)

            def take_probT(g, t):
                act.wait_ge(pt_done, TILES * g + t + 1)
                wait(act, o_done, TILES * g + t - 1)
                for h in range(2):
                    for a in range(2):
                        act.activation(probT[a * NODES:(a + 1) * NODES, t % 2, :, h, a, :],
                                       ps_probT[h * NODES:(h + 1) * NODES, t % 2, :, a * NODES:(a + 1) * NODES],
                                       ACT.Copy).then_inc(probT_done, 1)

            def att_hi(g, t):
                act.wait_ge(o_done, TILES * g + t + 1)
                wait(act, proj_done, TILES * g + t - 1)
                act.activation(attT_hi[:, t % 2], lin[bank_of(g, "O", t)][:, :], ACT.Copy)\
                   .then_inc(att_hi_done, 1)

            def body(g, par):
                def unit(j):
                    if "U" in kinds_of(g):
                        take = take_q if j % 3 == 0 else take_k
                        take(g + 1, 1 - par, j // 3, bank_of(g, "U", j))
                unit(0)
                exponent(g, 0)
                unit(1)
                exponent(g, 1)
                take_probT(g, 0)
                unit(3)
                if is_last(g):
                    split_hi(0)
                exponent(g, 2)
                att_hi(g, 0)
                unit(4)
                take_probT(g, 1)
                exponent(g, 3)
                if is_last(g):
                    split_hi(1)
                unit(6)
                att_hi(g, 1)
                take_probT(g, 2)
                unit(7)
                att_hi(g, 2)
                take_probT(g, 3)
                unit(9)
                unit(10)
                if is_last(g):
                    for k in range(KC):
                        mlp_affine(0, k)
                att_hi(g, 3)
                if "T" in kinds_of(g):
                    for k in range(KC):
                        affine(g + 2, k, bank_of(g, "T", k))

            def split_hi(n):
                act.wait_ge(raw_loaded[n % RAW], 16 * (n // RAW + 1))
                source, _, hi, _ = piece_views(n)
                act.activation(hi, source, ACT.Copy).then_inc(piece_hi, 1)

            def mlp_affine(g, k):
                act.wait_ge(mlp_t_done, KC * g + k + 1)
                wait(act, mlp_nx_split, KC * g + k - 1)
                act.activation(mlp_nxT[:, k % 2], ps_t[k % 2][:, :], ACT.Identity, scale=mlp_cols[:, 0, k:k + 1],
                               bias=mlp_cols[:, 1, k:k + 1]).then_inc(mlp_nx_done, 1)

            def mlp_body(g):
                for m in range(FC):
                    n = FC * g + m
                    act.wait_ge(up_done, n + 1)
                    wait(act, h_split, n - 1)
                    act.activation(hT[:, m % 2], ps_h[m % 2][:, :], ACT.Gelu,
                                   bias=b1_cols[:, m:m + 1]).then_inc(gelu_done, 1)
                    if is_first(g) and m == 0:
                        act.wait_ge(proj_done, TILES * NG)
                        act.wait_ge(x1_done, TILES * NG)
                    act.wait_ge(gelu_done, n + 1)
                    wait(act, down_done, n - HR + 1)
                    act.activation(hT_hi[:, m % HR], hT[:, m % 2], ACT.Copy).then_inc(h_hi_done, 1)
                    if is_first(g) and m + LAG < len(PIECES):
                        if m == 3:
                            for i in range(2):
                                act.wait_ge(x1_stored[i], 16 * 2 * NG)
                        split_hi(m + LAG)
                if not isinstance(g, int) or g + 1 < NG:
                    for k in range(KC):
                        mlp_affine(g + 1, k)

            weight_hi(0)
            act.wait_ge(cols_loaded, 16 * 7)
            affine(0, 0, bank_of(-2, "T", 0))
            affine(0, 1, bank_of(-2, "T", 1))
            weight_hi(1)
            affine(0, 2, bank_of(-2, "T", 2))
            affine(0, 3, bank_of(-2, "T", 3))
            weight_hi(2)
            act.dma_start(bv_all[:, :], bv.partition_broadcast(P)).then_inc(rows_loaded, 16)
            act.dma_start(bo_all[:, :], bo.partition_broadcast(P)).then_inc(rows_loaded, 16)
            act.wait_ge(k_zeroed, 2)
            for m in range(KC):
                take_q(0, 0, m, bank_of(-1, "U", 3 * m))
                take_k(0, 0, m, bank_of(-1, "U", 3 * m + 1))
            weight_hi(3)
            for k in range(KC):
                affine(1, k, bank_of(-1, "T", k))
            for i in range(4):
                act.wait_ge(w_lo_done[i], 1)
            body(0, 0)
            with act.Fori(1, NG - 4, 2) as g:
                body(g, 1)
                body(g + 1, 0)
            for g in range(NG - 3, NG):
                body(g, g % 2)
            mlp_body(0)
            with act.Fori(1, NG - 2, 2) as g:
                mlp_body(g)
                mlp_body(g + 1)
            mlp_body(NG - 1)

        @block.vector
        def _(dve):
            def weight_lo(i):
                dve.wait_ge(w_hi_done[i], 1)
                dve.tensor_tensor(w_lo[i][:, :, :], raw_w[i], w_hi[i][:, :, :].bitcast(F32),
                                  ALU.subtract).then_inc(w_lo_done[i], 1)

            def ln_stats(g, par, t):
                if is_first(g):
                    dve.wait_ge(x0_loaded[t], 16)
                elif t == 0:
                    dve.wait_ge(x_loaded[par], 8 * (g + par))
                dve.bn_stats(stats[:, t, :], x[par][:, t, :]).then_inc(stats_done, 1)

            def ln_var(g):
                wait_apart(dve, stats_done, TILES * (g + 1), stats_passed)
                for t in range(TILES):
                    dve.bn_aggr(moments[:, t, :], stats[:, t, :]).then_inc(moments_done, 1)
                dve.wait_ge(moments_done, TILES * (g + 1))
                dve.tensor_scalar(var_eps[:, :], moments[:, :, 1], EPS, None, ALU.add).then_inc(var_done, 1)

            def ln_norm(g, par, t):
                dve.wait_ge(rstd_done, g + 1)
                dve.tensor_scalar(x[par][:, t, :], x[par][:, t, :], moments[:, t, 0:1], rstd[:, t:t + 1],
                                  ALU.subtract, ALU.mult).then_inc(zn_done, 1)

            def split_nx(g, k):
                dve.wait_ge(nx_done, KC * g + k + 1)
                wait(dve, u_done, UNITS * g)
                dve.tensor_copy(nxT_hi[:, k], nxT[:, k % 2]).then_inc(nx_hi_done, 1)
                dve.wait_ge(nx_hi_done, KC * g + k + 1)
                dve.tensor_tensor(nxT_lo[:, k], nxT[:, k % 2], nxT_hi[:, k].bitcast(F32),
                                  ALU.subtract).then_inc(nx_split, 1)

            def take_v(g, par, t, bank):
                dve.wait_ge(u_done, UNITS * g + 3 * t + 3)
                dve.tensor_tensor(v[par][:, t, :], lin[bank][:, :], bv_all[:, :], ALU.add).then_inc(v_done, 1)

            def mask_and_shift(g, par, t):
                n = TILES * g + t
                if t == 0:
                    dve.wait_ge(mask_loaded[par], 8 * (g - par) + 16)
                dve.wait_ge(neg_filled, n + 1)
                wait_apart(dve, s_done, n + 1, mask_passed)
                flags = mask[:, par, t, :].unsqueeze(1).broadcast_to((P, HEADS, NODES))
                dve.copy_predicated(scores[:, t % 2], flags, ps_scores[:, t % 2]).then_inc(masked, 1)
                dve.wait_ge(masked, n + 1)
                dve.tensor_reduce(row_max[:, :], scores[:, t % 2], AX.X, ALU.max).then_inc(max_done, 1)
                dve.wait_ge(max_done, n + 1)
                dve.tensor_tensor(scores[:, t % 2], scores[:, t % 2],
                                  row_max[:, :].unsqueeze(2).broadcast_to((P, HEADS, NODES)),
                                  ALU.subtract).then_inc(shifted, 1)

            def normalise(g, t):
                n = TILES * g + t
                dve.wait_ge(exp_done, n + 1)
                dve.tensor_reduce(row_sum[:, :], expd[:, t % 2], AX.X, ALU.add).then_inc(sum_done, 1)
                dve.wait_ge(sum_done, n + 1)
                dve.reciprocal(row_inv[:, :], row_sum[:, :]).then_inc(inv_done, 1)
                dve.wait_ge(inv_done, n + 1)
                wait(dve, pt_done, n - 1)
                dve.tensor_tensor(prob[:, t % 2], expd[:, t % 2],
                                  row_inv[:, :].unsqueeze(2).broadcast_to((P, HEADS, NODES)),
                                  ALU.mult).then_inc(prob_done, 1)

            def att_lo(g, t):
                bank = bank_of(g, "O", t)
                n = TILES * g + t
                dve.wait_ge(att_hi_done, n + 1)
                dve.tensor_tensor(attT_lo[:, t % 2], lin[bank][:, :], attT_hi[:, t % 2].bitcast(F32),
                                  ALU.subtract).then_inc(att_split, 1)

            def residual(g, t):
                bank = bank_of(g, "W", t)
                n = TILES * g + t
                dve.wait_ge(proj_done, n + 1)
                dve.wait_ge(xres_biased, n + 1)
                dve.tensor_tensor(xres[:, t % 2], lin[bank][:, :], xres[:, t % 2], ALU.add).then_inc(x1_done, 1)

            def body(g, par):
                def unit_v(t):
                    if "U" in kinds_of(g):
                        take_v(g + 1, 1 - par, t, bank_of(g, "U", 3 * t + 2))
                ln = "T" in kinds_of(g)
                mask_and_shift(g, par, 0)
                if ln:
                    ln_stats(g + 2, par, 0)
                    ln_stats(g + 2, par, 1)
                normalise(g, 0)
                mask_and_shift(g, par, 1)
                unit_v(0)
                if ln:
                    ln_stats(g + 2, par, 2)
                    ln_stats(g + 2, par, 3)
                    ln_var(g + 2)
                if is_last(g):
                    for n in range(TILES):
                        mlp_ln_stats(0, 0, n)
                    mlp_ln_var(0)
                normalise(g, 1)
                mask_and_shift(g, par, 2)
                att_lo(g, 0)
                if ln:
                    ln_norm(g + 2, par, 0)
                    ln_norm(g + 2, par, 1)
                unit_v(1)
                normalise(g, 2)
                mask_and_shift(g, par, 3)
                residual(g, 0)
                if ln:
                    ln_norm(g + 2, par, 2)
                    ln_norm(g + 2, par, 3)
                att_lo(g, 1)
                if is_last(g):
                    for n in range(TILES):
                        mlp_ln_norm(0, 0, n)
                normalise(g, 3)
                residual(g, 1)
                att_lo(g, 2)
                unit_v(2)
                residual(g, 2)
                if is_last(g):
                    for k in range(KC):
                        mlp_split_nx(0, k)
                att_lo(g, 3)
                unit_v(3)
                if ln:
                    for k in range(KC):
                        split_nx(g + 2, k)
                residual(g, 3)

            def mlp_ln_stats(g, par, t):
                if t == 0:
                    dve.wait_ge(x1_loaded[par], 8 * (g - par) + 16)
                dve.bn_stats(stats[:, t, :], x1[par][:, t, :]).then_inc(mlp_stats_done, 1)

            def mlp_ln_var(g):
                wait_apart(dve, mlp_stats_done, TILES * (g + 1), mlp_stats_passed)
                for t in range(TILES):
                    dve.bn_aggr(moments[:, t, :], stats[:, t, :]).then_inc(mlp_moments_done, 1)
                dve.wait_ge(mlp_moments_done, TILES * (g + 1))
                dve.tensor_scalar(var_eps[:, :], moments[:, :, 1], EPS, None, ALU.add).then_inc(mlp_var_done, 1)

            def mlp_ln_norm(g, par, t):
                dve.wait_ge(mlp_rstd_done, g + 1)
                wait(dve, mlp_t_done, KC * g)
                dve.tensor_scalar(zn[:, t, :], x1[par][:, t, :], moments[:, t, 0:1], rstd[:, t:t + 1],
                                  ALU.subtract, ALU.mult).then_inc(mlp_zn_done, 1)

            def mlp_split_nx(g, k):
                dve.wait_ge(mlp_nx_done, KC * g + k + 1)
                wait(dve, up_done, FC * g)
                dve.tensor_copy(mlp_nxT_hi[:, k], mlp_nxT[:, k % 2]).then_inc(mlp_nx_hi_done, 1)
                dve.wait_ge(mlp_nx_hi_done, KC * g + k + 1)
                dve.tensor_tensor(mlp_nxT_lo[:, k], mlp_nxT[:, k % 2], mlp_nxT_hi[:, k].bitcast(F32),
                                  ALU.subtract).then_inc(mlp_nx_split, 1)

            def mlp_body(g, par):
                more = not isinstance(g, int) or g + 1 < NG
                for m in range(FC):
                    dve.wait_ge(h_hi_done, FC * g + m + 1)
                    dve.tensor_tensor(hT_lo[:, m % HR], hT[:, m % 2], hT_hi[:, m % HR].bitcast(F32),
                                      ALU.subtract).then_inc(h_split, 1)
                    if more and 3 <= m < 3 + TILES:
                        mlp_ln_stats(g + 1, 1 - par, m - 3)
                    if more and m == 3 + TILES:
                        mlp_ln_var(g + 1)
                    if more and 9 <= m < 9 + TILES:
                        mlp_ln_norm(g + 1, 1 - par, m - 9)
                if more:
                    for k in range(KC):
                        mlp_split_nx(g + 1, k)
                dve.wait_ge(down_done, FC * (g + 1))
                for t in range(TILES):
                    dve.wait_ge(x1_biased, TILES * g + t + 1)
                    dve.tensor_tensor(x1[par][:, t, :], ps_out[t][:, :], x1[par][:, t, :], ALU.add)\
                       .then_inc(out_done, 1)

            for g in range(2):
                for t in range(TILES):
                    ln_stats(g, g, t)
                ln_var(g)
                for t in range(TILES):
                    ln_norm(g, g, t)
                if g == 0:
                    weight_lo(0)
                    for k in range(KC):
                        split_nx(0, k)
                    weight_lo(2)
            dve.wait_ge(rows_loaded, 16 * 2)
            for t in range(TILES):
                take_v(0, 0, t, bank_of(-1, "U", 3 * t + 2))
            weight_lo(3)
            for k in range(KC):
                split_nx(1, k)
            dve.wait_ge(w_lo_done[1], 1)
            dve.wait_ge(probT_zeroed, 2)
            body(0, 0)
            with dve.Fori(1, NG - 4, 2) as g:
                body(g, 1)
                body(g + 1, 0)
            for g in range(NG - 3, NG):
                body(g, g % 2)
            mlp_body(0, 0)
            with dve.Fori(1, NG - 2, 2) as g:
                mlp_body(g, 1)
                mlp_body(g + 1, 0)
            mlp_body(NG - 1, 1)

        @block.tensor
        def _(pe):
            def take_bank(g, kind, n):
                bank, last = ring_place(g, kind, n)
                if last is not None:
                    i, kind, n = last
                    which = {"U": (q_done, k_done, v_done)[n % 3], "T": nx_done, "O": att_split, "W": x1_done}[kind]
                    if kind == "U":
                        per = 2 if n % 3 == 1 else 1
                        pe.wait_ge(which, per * (KC * (i + 1) + n // 3 + 1))
                    elif kind == "T":
                        pe.wait_ge(which, KC * (i + 2) + n + 1)
                    else:
                        pe.wait_ge(which, TILES * i + n + 1)
                return lin[bank]

            def transposes(g, par, k, bank):
                pe.wait_ge(zn_done, TILES * (g + 1))
                for t in range(TILES):
                    mm = pe.transpose(bank[:, t * P:(t + 1) * P], x[par][:, t, k * P:(k + 1) * P], ident[:, :])
                mm.then_inc(t_done, 1)

            def unit(g, j, bank):
                m, which = j // 3, j % 3
                if is_first(g) and m == 0:
                    pe.wait_ge(w_lo_done[which], 1)
                for c in range(KC):
                    if j == 0:
                        pe.wait_ge(nx_split, KC * g + c + 1)
                    nx = (nxT_hi[:, c, :], nxT_lo[:, c, :])
                    if which < 2:
                        lhs = tuple(w[which][:, c, m * P:(m + 1) * P] for w in (w_hi, w_lo))
                        rhs = nx
                    else:
                        lhs = tuple(n[:, m * P:(m + 1) * P] for n in nx)
                        rhs = tuple(w[2][:, c, :] for w in (w_hi, w_lo))
                    mm = split3(pe, bank[:, :], lhs, rhs, c == 0, c == KC - 1)
                mm.then_inc(u_done, 1)

            def score(g, par, t):
                n = TILES * g + t
                if t == 0:
                    pe.wait_ge(q_done, KC * (g + 1))
                    pe.wait_ge(k_done, 2 * KC * (g + 1))
                wait(pe, masked, n - 1)
                for m in range(KC):
                    for a in range(2):
                        mm = pe.matmul(ps_scores[a * NODES:(a + 1) * NODES, t % 2, 2 * m:2 * m + 2, :],
                                       qT[par][:, m, t * P + a * NODES:t * P + (a + 1) * NODES],
                                       kT[par][:, t, m, a, :, :], start=True, stop=True)
                mm.then_inc(s_done, 1)

            def prob_transposes(g, t):
                n = TILES * g + t
                pe.wait_ge(prob_done, n + 1)
                wait(pe, probT_done, 4 * (n - 1))
                for m in range(KC):
                    mm = pe.transpose(ps_probT[:, t % 2, m, :], prob[:, t % 2, 2 * m:2 * m + 2, :], ident[:, :])
                mm.then_inc(pt_done, 1)

            def attend(g, par, t, bank):
                pe.wait_ge(probT_done, 4 * (TILES * g + t + 1))
                if t == 0:
                    pe.wait_ge(v_done, TILES * (g + 1))
                for h in range(HEADS):
                    rows = slice((h % 2) * HD, (h % 2 + 1) * HD)
                    mm = pe.matmul(bank[rows, (h // 2) * P:(h // 2 + 1) * P], v[par][:, t, h * HD:(h + 1) * HD],
                                   probT[:, t % 2, h // 2, h % 2, :, :], start=True, stop=True)
                mm.then_inc(o_done, 1)

            def project(g, t, bank):
                if is_first(g) and t == 0:
                    pe.wait_ge(w_lo_done[3], 1)
                pe.wait_ge(att_split, TILES * g + t + 1)
                for c in range(KC):
                    mm = split3(pe, bank[:, :], tuple(a[:, t % 2, c * P:(c + 1) * P] for a in (attT_hi, attT_lo)),
                                tuple(w[3][:, c, :] for w in (w_hi, w_lo)), c == 0, c == KC - 1)
                mm.then_inc(proj_done, 1)

            def body(g, par):
                for kind, n in order_of(g):
                    if kind == "S":
                        score(g, par, n)
                    elif kind == "P":
                        prob_transposes(g, n)
                        if is_last(g) and n == TILES - 1:
                            pe.wait_ge(masked, TILES * NG)
                            mlp_transposes(0)
                    elif kind == "U":
                        unit(g + 1, n, take_bank(g, "U", n))
                    elif kind == "O":
                        attend(g, par, n, take_bank(g, "O", n))
                    elif kind == "W":
                        project(g, n, take_bank(g, "W", n))
                    else:
                        transposes(g + 2, par, n, take_bank(g, "T", n))

            def mlp_transposes(g, chunks=range(KC)):
                pe.wait_ge(mlp_zn_done, TILES * (g + 1))
                for k in chunks:
                    wait(pe, mlp_nx_done, KC * g + k - 1)
                    for t in range(TILES):
                        mm = pe.transpose(ps_t[k % 2][:, t * P:(t + 1) * P], zn[:, t, k * P:(k + 1) * P],
                                          ident[:, :])
                    mm.then_inc(mlp_t_done, 1)

            def up(g, m):
                n = FC * g + m
                wait(pe, gelu_done, n - 1)
                if is_first(g) and m % 2 == 0:
                    pe.wait_ge(piece_lo, PIECES.index((1, m // 2)) + 1)
                for c in range(KC):
                    if m == 0:
                        pe.wait_ge(mlp_nx_split, KC * g + c + 1)
                    mm = split3(pe, ps_h[m % 2][:, :], tuple(w[:, c, m * P:(m + 1) * P] for w in (w1_hi, w1_lo)),
                                (mlp_nxT_hi[:, c, :], mlp_nxT_lo[:, c, :]), c == 0, c == KC - 1)
                mm.then_inc(up_done, 1)

            def down(g, m):
                pe.wait_ge(h_split, FC * g + m + 1)
                if m == 0:
                    wait(pe, out_done, TILES * g)
                if m == 0 and is_first(g):
                    pe.wait_ge(x1_done, TILES * NG)
                if is_first(g) and m % 2 == 0:
                    pe.wait_ge(piece_lo, PIECES.index((2, m // 2)) + 1)
                for t in range(TILES):
                    mm = split3(pe, ps_out[t][:, :], tuple(h[:, m % HR, t * P:(t + 1) * P] for h in (hT_hi, hT_lo)),
                                (w2_hi[:, m, :], w2_lo[:, m, :]), m == 0, m == FC - 1)
                mm.then_inc(down_done, 1)

            def mlp_body(g):
                for m in range(FC):
                    up(g, m)
                    if m >= LAG and m < FC - 1:
                        down(g, m - LAG)
                more = not isinstance(g, int) or g + 1 < NG
                if more:
                    mlp_transposes(g + 1, (0, 1))
                down(g, FC - 3)
                if more:
                    mlp_transposes(g + 1, (2, 3))
                down(g, FC - 2)
                down(g, FC - 1)

            pe.wait_ge(ident_done, 1)
            body(-2, 0)
            body(-1, 1)
            body(0, 0)
            with pe.Fori(1, NG - 4, 2) as g:
                body(g, 1)
                body(g + 1, 0)
            for g in range(NG - 3, NG):
                body(g, g % 2)
            pe.wait_ge(probT_done, 4 * TILES * NG)
            mlp_body(0)
            with pe.Fori(1, NG - 2, 2) as g:
                mlp_body(g)
                mlp_body(g + 1)
            mlp_body(NG - 1)


_INS = ["x", "adj"] + [f"L0_gnn_{n}" for n in ("ln1_g", "ln1_b", "ln2_g", "ln2_b", "Wq", "bq", "Wk", "bk", "Wv", "bv",
                                               "Wo", "bo", "W1", "b1", "W2", "b2")]


def kernel(**inputs):
    import numpy as np
    import concourse.bacc as bacc
    from concourse.bass_utils import run_bass_kernel_spmd

    nc = bacc.Bacc("TRN2", target_bir_lowering=False, num_devices=1)
    arrays, args = {}, []
    for name in _INS:
        a = np.ascontiguousarray(inputs[name])
        if name == "x":
            a = a.reshape(TOKENS, HID)
        arrays[f"in_{name}"] = a
        args.append(nc.dram_tensor(f"in_{name}", a.shape, mybir.dt.from_np(a.dtype), kind="ExternalInput").ap())
    out = nc.dram_tensor("out", (TOKENS, HID), F32, kind="ExternalOutput").ap()
    adj_layer(nc, *args, out)
    r = run_bass_kernel_spmd(nc, [arrays], core_ids=[0])
    return r.results[0]["out"].reshape(GRAPHS, NODES, HID)
```

```python
from contextlib import ExitStack

import concourse.bass as bass
from concourse import mybir

F32 = mybir.dt.float32
F32R = mybir.dt.float32r
U8 = mybir.dt.uint8
ALU = mybir.AluOpType
ACT = mybir.ActivationFunctionType
AX = mybir.AxisListType

P = 128
GRAPHS, NODES, HID = 128, 64, 512
HEADS = 8
HD = HID // HEADS
FF = 4 * HID
TOKENS = GRAPHS * NODES
KC = HID // P
FC = FF // P
TILES = 4
GT = TILES * P
NG = TOKENS // GT
EPS = 1e-5
SCALE = HD ** -0.5
NEG = -1.0e9 / SCALE

UNITS = 3 * KC
ORDER = [("S", 0), ("U", 0), ("U", 1), ("S", 1), ("U", 2), ("P", 0), ("U", 3), ("S", 2), ("O", 0), ("U", 4),
         ("P", 1), ("U", 5), ("S", 3), ("W", 0), ("U", 6), ("O", 1), ("P", 2), ("U", 7), ("W", 1), ("O", 2),
         ("U", 8), ("P", 3), ("U", 9), ("W", 2), ("O", 3), ("U", 10), ("U", 11), ("W", 3)]
FIRST_UNITS = [3 * m + which for which in range(3) for m in range(KC)]
LATE_UNITS = [3 * t + 2 for t in range(TILES)]
LAST_ORDER = [("S", 0), ("L", 2), ("S", 1), ("L", 5), ("P", 0), ("S", 2), ("L", 8), ("O", 0), ("P", 1), ("S", 3),
              ("L", 11), ("O", 1), ("W", 0), ("P", 2), ("W", 1), ("O", 2), ("P", 3), ("M", 0), ("M", 1),
              ("W", 2), ("M", 2), ("M", 3), ("O", 3), ("F", 0), ("W", 3)]
LIN = 4

WCH = 8
PIECES = [(1, 0)] + [p for c in range(1, WCH) for p in ((1, c), (2, c - 1))] + [(2, WCH - 1)]
RAW = 2
BLK = 32
QUADS = P // BLK
HR = 4
LAG = 2


def kinds_of(g):
    if not isinstance(g, int):
        return "SPOWUN"
    return ("SPOW" if g >= 0 else "") + ("U" if 0 <= g + 1 < NG else "") + ("N" if 0 <= g < NG - 2 else "")


def order_of(g):
    if isinstance(g, int) and g < 0:
        return [("U", j) for j in FIRST_UNITS if g == -1] + [("T", k) for k in range(KC)]
    if is_last(g):
        return LAST_ORDER
    late = LATE_UNITS if isinstance(g, int) and g == NG - 2 else []
    return [(k, n) for k, n in ORDER if k in kinds_of(g) and not (k == "U" and n in late)]


def units_through(g, j):
    order = FIRST_UNITS if is_first(g) else list(range(UNITS))
    if is_last(g):
        order = [i for i in order if i not in LATE_UNITS] + LATE_UNITS
    return UNITS * g + order.index(j) + 1


def lin_uses(g):
    return [(g, k, n) for k, n in order_of(g) if k in "UTOWL"]


def ring_place(g, kind, n):
    if isinstance(g, int):
        uses = [u for i in range(-2, g + 1) for u in lin_uses(i)]
        at = uses.index((g, kind, n))
        return at % LIN, uses[at - LIN] if at >= LIN else None
    uses = lin_uses(g)
    at = [u[1:] for u in uses].index((kind, n))
    assert len(uses) % LIN == 0 and len(lin_uses(-2) + lin_uses(-1) + lin_uses(0)) % LIN == 0
    return at % LIN, uses[at - LIN] if at >= LIN else (g - 1, *uses[at - LIN][1:])


def bank_of(g, kind, n):
    return ring_place(g, kind, n)[0]


def wait(eng, sem, value):
    if not isinstance(value, int) or value > 0:
        eng.wait_ge(sem, value)


def is_first(g):
    return isinstance(g, int) and g == 0


def is_last(g):
    return isinstance(g, int) and g == NG - 1


def wait_apart(eng, sem, value, passed):
    wait(eng, sem, value)
    if not isinstance(value, int):
        eng.sem_inc(passed, 1)


def split3(pe, out, lhs, rhs, first, last):
    pe.matmul(out, lhs[1], rhs[0], start=first, stop=False)
    pe.matmul(out, lhs[0], rhs[1], start=False, stop=False)
    return pe.matmul(out, lhs[0], rhs[0], start=False, stop=last)


def adj_layer(nc, x_dram, adj, ln1_g, ln1_b, ln2_g, ln2_b, wq, bq, wk, bk, wv, bv, wo, bo, w1, b1, w2, b2, out_dram):
    x1_dram = nc.dram_tensor("x1_scratch", (TOKENS, HID), F32, kind="Internal").ap()
    x_groups, x1_groups = (a.rearrange("(g t p) n -> g p t n", t=TILES, p=P) for a in (x_dram, x1_dram))
    x_tiles, x1_tiles, out_tiles = (a.rearrange("(n p) d -> n p d", p=P) for a in (x_dram, x1_dram, out_dram))
    adj_groups = adj.rearrange("(g t a) q k -> g (a q) t k", t=TILES, a=2)
    w1_cols, w2_rows = (a.rearrange("(c p) n -> p c n", p=P) for a in (w1, w2))

    ctx = ExitStack()
    with ctx:
        def placer(stack):
            return lambda name, shape, dt=F32: stack.enter_context(nc.sbuf_tensor(name, shape, dt))

        def sem(name):
            return ctx.enter_context(nc.semaphore(name))

        sb = placer(ctx)
        ident = sb("ident", [P, P])
        minus_half = sb("minus_half", [P, TILES])
        cols = sb("cols", [P, 4, KC])
        mlp_cols = sb("mlp_cols", [P, 2, KC])
        b1_cols = sb("b1_cols", [P, FC])
        stats = sb("stats", [P, TILES, 6])
        moments = sb("moments", [P, TILES, 2])
        var_eps = sb("var_eps", [P, TILES])
        rstd = sb("rstd", [P, TILES])
        row_max = sb("row_max", [P, HEADS])
        row_sum = sb("row_sum", [P, HEADS])
        row_inv = sb("row_inv", [P, HEADS])
        start = nc.sbuf_base

        with ExitStack() as phase:
            sb = placer(phase)
            wqkv_hi, wqkv_lo = ([sb(f"w{c}_{s}", [P, KC, HID], F32R) for c in "qkv"] for s in ("hi", "lo"))
            nxT_hi = sb("nxT_hi", [P, KC, GT], F32R)
            nxT_lo = sb("nxT_lo", [P, KC, GT], F32R)
            z1T = sb("z1T", [P, KC, GT])
            x = [sb(f"x{i}", [P, TILES, HID]) for i in range(2)]
            qT0 = sb("qT0", [P, KC, GT])
            kT0 = sb("kT0", [P, TILES, KC, 2, 2, NODES])
            v0 = sb("v0", [P, TILES, HID])
            early_end = nc.sbuf_base
            wo_hi, wo_lo = (sb(f"wo_{s}", [P, KC, HID], F32R) for s in ("hi", "lo"))
            xres = sb("xres", [P, 2, HID])
            bv_all = sb("bv_all", [P, HID])
            bo_all = sb("bo_all", [P, HID])
            qT = [qT0, sb("qT1", [P, KC, GT])]
            kT = [kT0, sb("kT1", [P, TILES, KC, 2, 2, NODES])]
            v = [v0, sb("v1", [P, TILES, HID])]
            softmax = sb("softmax", [P, 2, 2, HEADS, NODES])
            scores, expd = softmax[:, 0], softmax[:, 1]
            prob = sb("prob", [P, 2, HEADS, NODES])
            probT = sb("probT", [P, 2, KC, 2, 2, NODES])
            attT_hi = sb("attT_hi", [P, 2, HID], F32R)
            attT_lo = sb("attT_lo", [P, 2, HID], F32R)
            mask = sb("mask", [P, 2, TILES, NODES], U8)
            w_hi, w_lo = wqkv_hi + [wo_hi], wqkv_lo + [wo_lo]

        with ExitStack() as phase:
            sb = placer(phase)
            assert nc.sbuf_base == start
            w1_hi, w1_lo = (sb(f"w1_{s}", [P, KC, FF], F32R) for s in ("hi", "lo"))
            mlp_nxT_hi = sb("mlp_nxT_hi", [P, KC, GT], F32R)
            mlp_nxT_lo = sb("mlp_nxT_lo", [P, KC, GT], F32R)
            z2T = sb("z2T", [P, KC, GT])
            x1_0 = sb("x1_0", [P, TILES, HID])
            zn = sb("zn", [P, TILES, HID])
            raw = sb("raw", [P, RAW, KC * FF // WCH])
            hT = sb("hT", [P, 2, GT])
            assert nc.sbuf_base <= early_end
            w2_hi, w2_lo = (sb(f"w2_{s}", [P, FC, HID], F32R) for s in ("hi", "lo"))
            x1 = [x1_0, sb("x1_1", [P, TILES, HID])]
            hT_hi = sb("hT_hi", [P, HR, GT], F32R)
            hT_lo = sb("hT_lo", [P, HR, GT], F32R)
            b2_all = sb("b2_all", [P, HID])

        with ExitStack() as phase:
            lin = [phase.enter_context(nc.psum_tensor(f"lin{i}", [P, GT], F32)) for i in range(LIN)]
            ps_scores = phase.enter_context(nc.psum_tensor("ps_scores", [P, 2, HEADS, NODES], F32))
            ps_probT = phase.enter_context(nc.psum_tensor("ps_probT", [P, 2, KC, P], F32))
        with ExitStack() as phase:
            ps_out = [phase.enter_context(nc.psum_tensor(f"ps_out{i}", [P, HID], F32)) for i in range(TILES)]
            ps_t = [phase.enter_context(nc.psum_tensor(f"ps_t{i}", [P, GT], F32)) for i in range(2)]
            ps_h = [phase.enter_context(nc.psum_tensor(f"ps_h{i}", [P, GT], F32)) for i in range(2)]

        raw_w = [qT[1][:, :, :], v[1][:, :, :], softmax.rearrange("p s b h n -> p (s b) (h n)"), qT[1][:, :, :]]

        x0_loaded = [sem(f"x0_loaded{t}") for t in range(TILES)]
        x_loaded = [sem(f"x_loaded{i}") for i in range(2)]
        mask_loaded = [sem(f"mask_loaded{i}") for i in range(2)]
        xres_loaded = [sem(f"xres_loaded{i}") for i in range(2)]
        x1_stored = [sem(f"x1_stored{i}") for i in range(2)]
        w_loaded, w_hi_done, w_lo_done = ([sem(f"w{c}_{s}") for c in "qkvo"] for s in ("loaded", "hi_done", "lo_done"))
        cols_loaded, rows_loaded, mlp_cols_loaded = sem("cols_loaded"), sem("rows_loaded"), sem("mlp_cols_loaded")
        filled, ident_done = sem("filled"), sem("ident_done")
        k_zeroed, probT_zeroed = sem("k_zeroed"), sem("probT_zeroed")
        stats_done, moments_done, var_done = sem("stats_done"), sem("moments_done"), sem("var_done")
        rstd_done, zn_done, t_done = sem("rstd_done"), sem("zn_done"), sem("t_done")
        z_transposed = sem("z_transposed")
        nx_done, nx_hi_done, nx_split = sem("nx_done"), sem("nx_hi_done"), sem("nx_split")
        u_done, q_done, k_done, v_done = sem("u_done"), sem("q_done"), sem("k_done"), sem("v_done")
        s_done, neg_filled, masked, max_done = sem("s_done"), sem("neg_filled"), sem("masked"), sem("max_done")
        shifted, exp_done, sum_done, inv_done = sem("shifted"), sem("exp_done"), sem("sum_done"), sem("inv_done")
        prob_done, pt_done, probT_done = sem("prob_done"), sem("pt_done"), sem("probT_done")
        o_done, att_hi_done, att_split = sem("o_done"), sem("att_hi_done"), sem("att_split")
        mask_passed, fill_passed, stats_passed = sem("mask_passed"), sem("fill_passed"), sem("stats_passed")
        proj_done, xres_biased, x1_done = sem("proj_done"), sem("xres_biased"), sem("x1_done")
        x1_loaded = [sem(f"x1_loaded{i}") for i in range(2)]
        out_stored = [sem(f"out_stored{i}") for i in range(2)]
        raw_loaded = [sem(f"raw_loaded{i}") for i in range(RAW)]
        b2_loaded = sem("b2_loaded")
        piece_hi, piece_lo = sem("piece_hi"), sem("piece_lo")
        mlp_stats_done, mlp_moments_done, mlp_var_done = (sem(f"mlp_{s}_done") for s in ("stats", "moments", "var"))
        mlp_rstd_done, mlp_zn_done, mlp_t_done = (sem(f"mlp_{s}_done") for s in ("rstd", "zn", "t"))
        mlp_nx_done, mlp_nx_hi_done, mlp_nx_split = sem("mlp_nx_done"), sem("mlp_nx_hi_done"), sem("mlp_nx_split")
        mlp_stats_passed, zn_passed, first_t_done = sem("mlp_stats_passed"), sem("zn_passed"), sem("first_t_done")
        up_done, gelu_done, h_hi_done = sem("up_done"), sem("gelu_done"), sem("h_hi_done")
        h_split, down_done, tile_summed = sem("h_split"), sem("down_done"), sem("tile_summed")
        x1_biased, out_done = sem("x1_biased"), sem("out_done")

        def piece_views(n):
            which, c = PIECES[n]
            per, rows, source, hi, lo = ((FF // WCH, KC, w1_cols, w1_hi, w1_lo) if which == 1 else
                                         (FC // WCH, FC // WCH, w2_rows, w2_hi, w2_lo))
            cut = slice(c * per, (c + 1) * per)
            cut = (slice(None), slice(None), cut) if which == 1 else (slice(None), cut)
            return raw[:, n % RAW, :].rearrange("p (c n) -> p c n", c=rows), source[cut], hi[cut], lo[cut]

        block = ctx.enter_context(nc.Block())

        @block.sync
        def _(sp):
            def load_x(g, par):
                if isinstance(g, int) and g < 4:
                    wait(sp, t_done, KC * (g - 1))
                else:
                    sp.wait_ge(z_transposed, g - 3)
                sp.dma_start(x[par][:, :, :], x_groups[g]).then_inc(x_loaded[par], 16)

            def load_mask(g, par):
                with nc.allow_non_contiguous_dma(reason="rows of 64 flags"):
                    sp.dma_start(mask[:, par], adj_groups[g]).then_inc(mask_loaded[par], 16)

            def load_xres(g, t):
                wait(sp, x1_stored[t % 2], 16 * (2 * g + t // 2))
                sp.dma_start(xres[:, t % 2], x_tiles[g * TILES + t]).then_inc(xres_loaded[t % 2], 16)

            def store_x1(g, t):
                sp.wait_ge(x1_done, TILES * g + t + 1)
                sp.dma_start(x1_tiles[g * TILES + t], xres[:, t % 2]).then_inc(x1_stored[t % 2], 16)

            def body(g, par):
                if not isinstance(g, int) or g + 3 < NG:
                    load_x(g + 3, 1 - par)
                if "U" in kinds_of(g):
                    load_mask(g + 1, 1 - par)
                load_xres(g, 0)
                load_xres(g, 1)
                if is_last(g):
                    sp.wait_ge(proj_done, TILES * g)
                    load_x1(0, 0)
                    for n in range(RAW):
                        load_piece(n)
                store_x1(g, 0)
                load_xres(g, 2)
                store_x1(g, 1)
                load_xres(g, 3)
                if is_last(g):
                    load_piece(RAW)
                store_x1(g, 2)
                store_x1(g, 3)

            def load_piece(n):
                wait(sp, piece_lo, n - RAW + 1)
                to, source, _, _ = piece_views(n)
                sp.dma_start(to, source).then_inc(raw_loaded[n % RAW], 16)

            def load_x1(g, par):
                wait(sp, out_stored[par], 32 * (g - par) if not isinstance(g, int) else 64 * (g // 2))
                sp.dma_start(x1[par][:, :, :], x1_groups[g]).then_inc(x1_loaded[par], 16)

            def mlp_body(g, par):
                if not isinstance(g, int) or g + 1 < NG:
                    load_x1(g + 1, 1 - par)
                if is_first(g):
                    for n in range(RAW + 2, len(PIECES)):
                        load_piece(n)
                for t in range(TILES):
                    sp.wait_ge(out_done, TILES * g + t + 1)
                    sp.dma_start(out_tiles[g * TILES + t], x1[par][:, t, :]).then_inc(out_stored[par], 16)

            for t in range(TILES):
                sp.dma_start(x[0][:, t, :], x_tiles[t]).then_inc(x0_loaded[t], 16)
            for i, w in enumerate((wq, wk, wv)):
                sp.dma_start(raw_w[i], w.rearrange("(c p) n -> p c n", p=P)).then_inc(w_loaded[i], 16)
            load_x(1, 1)
            load_mask(0, 0)
            sp.wait_ge(w_lo_done[0], 2)
            sp.dma_start(raw_w[3], wo.rearrange("(c p) n -> p c n", p=P)).then_inc(w_loaded[3], 16)
            load_x(2, 0)
            body(0, 0)
            with sp.Fori(1, NG - 4, 2) as g:
                body(g, 1)
                body(g + 1, 0)
            for g in range(NG - 3, NG):
                body(g, g % 2)
            load_piece(RAW + 1)
            for i in range(2):
                sp.wait_ge(x1_stored[i], 16 * 2 * NG)
            sp.dma_start(b2_all[:, :], b2.partition_broadcast(P)).then_inc(b2_loaded, 16)
            mlp_body(0, 0)
            with sp.Fori(1, NG - 2, 2) as g:
                mlp_body(g, 1)
                mlp_body(g + 1, 0)
            mlp_body(NG - 1, 1)
            for i in range(2):
                sp.wait_ge(out_stored[i], 16 * TILES * NG // 2)

        @block.gpsimd
        def _(pool):
            pool.memset(ident[:, :], 0.0).then_inc(filled, 1)
            pool.memset(minus_half[:, :], -0.5).then_inc(filled, 1)
            pool.wait_ge(filled, 2)
            pool.affine_select(out=ident[:, :], in_=ident[:, :], compare_op=ALU.not_equal, fill=1.0,
                               base=0, pattern=[[-1, P]], channel_multiplier=1).then_inc(ident_done, 1)

            def rstd_of(g):
                pool.wait_ge(var_done, g + 1)
                pool.tensor_tensor(rstd[:, :], var_eps[:, :], minus_half[:, :], ALU.pow).then_inc(rstd_done, 1)

            def fill_neg(g, t):
                wait_apart(pool, exp_done, TILES * g + t - 1, fill_passed)
                pool.memset(scores[:, t % 2], NEG).then_inc(neg_filled, 1)

            def bias_xres(g, t):
                pool.wait_ge(xres_loaded[t % 2], 16 * (2 * g + t // 2 + 1))
                pool.tensor_tensor(xres[:, t % 2], xres[:, t % 2], bo_all[:, :], ALU.add).then_inc(xres_biased, 1)

            def body(g):
                fill_neg(g, 0)
                fill_neg(g, 1)
                bias_xres(g, 0)
                bias_xres(g, 1)
                fill_neg(g, 2)
                if "N" in kinds_of(g):
                    rstd_of(g + 2)
                fill_neg(g, 3)
                if is_last(g):
                    mlp_rstd(0)
                    split_lo(0)
                    split_lo(1)
                bias_xres(g, 2)
                bias_xres(g, 3)

            def mlp_rstd(g):
                pool.wait_ge(mlp_var_done, g + 1)
                pool.tensor_tensor(rstd[:, :], var_eps[:, :], minus_half[:, :], ALU.pow).then_inc(mlp_rstd_done, 1)

            def bias_x1(g, par, t):
                pool.wait_ge(mlp_zn_done, TILES * g + t + 1)
                pool.tensor_tensor(x1[par][:, t, :], x1[par][:, t, :], b2_all[:, :], ALU.add).then_inc(x1_biased, 1)

            def split_lo(n):
                pool.wait_ge(piece_hi, n + 1)
                source, _, hi, lo = piece_views(n)
                pool.tensor_tensor(lo, source, hi.bitcast(F32), ALU.subtract).then_inc(piece_lo, 1)

            def mlp_ln(g, par):
                mlp_rstd(g)
                for t in range(TILES):
                    bias_x1(g, par, t)

            def zero_kT(par):
                pool.memset(kT[par][:, :, :, :, :, :], 0.0).then_inc(k_zeroed, 1)

            def weight_lo(i, part):
                pool.wait_ge(w_hi_done[i], 1)
                pool.tensor_tensor(w_lo[i][:, part, :], raw_w[i][:, part], w_hi[i][:, part, :].bitcast(F32),
                                   ALU.subtract).then_inc(w_lo_done[i], 1)

            zero_kT(0)
            rstd_of(0)
            weight_lo(0, slice(KC // 2, KC))
            weight_lo(1, slice(0, KC))
            zero_kT(1)
            for par in range(2):
                pool.memset(probT[:, par], 0.0).then_inc(probT_zeroed, 1)
            rstd_of(1)
            pool.wait_ge(rows_loaded, 16 * 2)
            pool.wait_ge(w_lo_done[2], 1)
            body(0)
            with pool.Fori(1, NG - 4, 2) as g:
                body(g)
                body(g + 1)
            for g in range(NG - 3, NG):
                body(g)
            for m in range(FC):
                if m + LAG < len(PIECES):
                    split_lo(m + LAG)
                if m == 3:
                    mlp_rstd(1)
                if m == 7:
                    pool.wait_ge(b2_loaded, 16)
                if 7 <= m < 7 + TILES:
                    bias_x1(0, 0, m - 7)
                if 11 <= m < 11 + TILES:
                    bias_x1(1, 1, m - 11)
            with pool.Fori(1, NG - 2, 2) as g:
                mlp_ln(g + 1, 0)
                mlp_ln(g + 2, 1)

        @block.scalar
        def _(act):
            with nc.allow_non_contiguous_dma(reason="one value per channel"):
                for i, b in enumerate((ln1_g, ln1_b, bq, bk)):
                    act.dma_start(cols[:, i], b.rearrange("(c p) -> p c", p=P)).then_inc(cols_loaded, 16)

            def weight_hi(i):
                act.wait_ge(w_loaded[i], 16)
                act.activation(w_hi[i][:, :, :], raw_w[i], ACT.Copy).then_inc(w_hi_done[i], 1)

            def affine(g, k):
                source = z1T[:, k]
                if isinstance(g, int) and g < 2:
                    source = lin[bank_of(g - 2, "T", k)][:, :]
                    act.wait_ge(t_done, KC * g + k + 1)
                    wait(act, nx_split, KC * (g - 1) + k + 1)
                else:
                    act.wait_ge(z_transposed, g - 1)
                act.activation(z1T[:, k], source, ACT.Identity, scale=cols[:, 0, k:k + 1],
                               bias=cols[:, 1, k:k + 1]).then_inc(nx_done, 1)

            def nx_hi(g, k):
                act.wait_ge(nx_done, KC * g + k + 1)
                act.wait_ge(u_done, UNITS * g)
                act.activation(nxT_hi[:, k], z1T[:, k], ACT.Copy).then_inc(nx_hi_done, 1)

            def take_q(g, par, m, bank):
                act.wait_ge(u_done, units_through(g, 3 * m))
                act.activation(qT[par][:, m, :], lin[bank][:, :], ACT.Identity,
                               bias=cols[:, 2, m:m + 1]).then_inc(q_done, 1)

            def take_k(g, par, m, bank):
                act.wait_ge(u_done, units_through(g, 3 * m + 1))
                for h in range(2):
                    rows = slice(h * HD, (h + 1) * HD)
                    act.activation(kT[par][rows, :, m, :, h, :],
                                   lin[bank][rows, :].rearrange("p (t a n) -> p t a n", a=2, n=NODES), ACT.Identity,
                                   bias=cols[rows, 3, m:m + 1]).then_inc(k_done, 1)

            def exponent(g, t):
                act.wait_ge(shifted, TILES * g + t + 1)
                wait(act, prob_done, TILES * g + t - 1)
                act.activation(expd[:, t % 2], scores[:, t % 2], ACT.Exp, scale=SCALE).then_inc(exp_done, 1)

            def take_probT(g, t):
                act.wait_ge(pt_done, TILES * g + t + 1)
                wait(act, o_done, TILES * g + t - 1)
                for h in range(2):
                    for a in range(2):
                        act.activation(probT[a * NODES:(a + 1) * NODES, t % 2, :, h, a, :],
                                       ps_probT[h * NODES:(h + 1) * NODES, t % 2, :, a * NODES:(a + 1) * NODES],
                                       ACT.Copy).then_inc(probT_done, 1)

            def att_hi(g, t):
                act.wait_ge(o_done, TILES * g + t + 1)
                wait(act, proj_done, TILES * g + t - 1)
                act.activation(attT_hi[:, t % 2], lin[bank_of(g, "O", t)][:, :], ACT.Copy)\
                   .then_inc(att_hi_done, 1)

            def body(g, par):
                def unit(j):
                    if "U" in kinds_of(g):
                        take = take_q if j % 3 == 0 else take_k
                        take(g + 1, 1 - par, j // 3, bank_of(g, "U", j))
                unit(0)
                exponent(g, 0)
                unit(1)
                exponent(g, 1)
                take_probT(g, 0)
                unit(3)
                exponent(g, 2)
                att_hi(g, 0)
                unit(4)
                take_probT(g, 1)
                exponent(g, 3)
                unit(6)
                att_hi(g, 1)
                take_probT(g, 2)
                unit(7)
                att_hi(g, 2)
                take_probT(g, 3)
                unit(9)
                att_hi(g, 3)
                unit(10)
                if "N" in kinds_of(g):
                    for k in range(KC):
                        affine(g + 2, k)
                    for k in range(KC):
                        nx_hi(g + 2, k)

            def last_body(g):
                exponent(g, 0)
                exponent(g, 1)
                take_probT(g, 0)
                exponent(g, 2)
                att_hi(g, 0)
                take_probT(g, 1)
                exponent(g, 3)
                att_hi(g, 1)
                act.wait_ge(u_done, UNITS * NG)
                split_hi(0)
                take_probT(g, 2)
                split_hi(1)
                att_hi(g, 2)
                take_probT(g, 3)
                act.wait_ge(mlp_cols_loaded, 16 * 3)
                for k in range(KC):
                    mlp_affine(0, k)
                att_hi(g, 3)

            def split_hi(n):
                act.wait_ge(raw_loaded[n % RAW], 16 * (n // RAW + 1))
                source, _, hi, _ = piece_views(n)
                act.activation(hi, source, ACT.Copy).then_inc(piece_hi, 1)

            def mlp_affine(g, k):
                if is_first(g):
                    act.wait_ge(first_t_done, k + 1)
                else:
                    act.wait_ge(mlp_t_done, g)
                act.activation(z2T[:, k], ps_t[k % 2][:, :] if is_first(g) else z2T[:, k], ACT.Identity,
                               scale=mlp_cols[:, 0, k:k + 1],
                               bias=mlp_cols[:, 1, k:k + 1]).then_inc(mlp_nx_done, 1)

            def mlp_body(g):
                for m in range(FC):
                    n = FC * g + m
                    act.wait_ge(up_done, n + 1)
                    wait(act, h_split, n - 1)
                    act.activation(hT[:, m % 2], ps_h[m % 2][:, :], ACT.Gelu,
                                   bias=b1_cols[:, m:m + 1]).then_inc(gelu_done, 1)
                    if is_first(g) and m == 0:
                        act.wait_ge(proj_done, TILES * NG)
                        act.wait_ge(x1_done, TILES * NG)
                    act.wait_ge(gelu_done, n + 1)
                    wait(act, down_done, n - HR + 1)
                    act.activation(hT_hi[:, m % HR], hT[:, m % 2], ACT.Copy).then_inc(h_hi_done, 1)
                    if is_first(g) and m + LAG < len(PIECES):
                        if m == 3:
                            for i in range(2):
                                act.wait_ge(x1_stored[i], 16 * 2 * NG)
                        split_hi(m + LAG)
                if not isinstance(g, int) or g + 1 < NG:
                    for k in range(KC):
                        mlp_affine(g + 1, k)

            weight_hi(0)
            act.wait_ge(cols_loaded, 16 * 4)
            for k in range(KC):
                affine(0, k)
            weight_hi(1)
            act.dma_start(bv_all[:, :], bv.partition_broadcast(P)).then_inc(rows_loaded, 16)
            act.dma_start(bo_all[:, :], bo.partition_broadcast(P)).then_inc(rows_loaded, 16)
            with nc.allow_non_contiguous_dma(reason="one value per channel"):
                for to, b in ((mlp_cols[:, 0], ln2_g), (mlp_cols[:, 1], ln2_b), (b1_cols[:, :], b1)):
                    act.dma_start(to, b.rearrange("(c p) -> p c", p=P)).then_inc(mlp_cols_loaded, 16)
            weight_hi(2)
            for m in range(KC):
                take_q(0, 0, m, bank_of(-1, "U", 3 * m))
            weight_hi(3)
            act.wait_ge(k_zeroed, 1)
            for m in range(KC):
                take_k(0, 0, m, bank_of(-1, "U", 3 * m + 1))
            for k in range(KC):
                affine(1, k)
                nx_hi(1, k)
            for i in range(4):
                act.wait_ge(w_lo_done[i], 2 if i == 0 else 1)
            act.wait_ge(k_zeroed, 2)
            body(0, 0)
            with act.Fori(1, NG - 4, 2) as g:
                body(g, 1)
                body(g + 1, 0)
            for g in range(NG - 3, NG - 1):
                body(g, g % 2)
            last_body(NG - 1)
            mlp_body(0)
            with act.Fori(1, NG - 2, 2) as g:
                mlp_body(g)
                mlp_body(g + 1)
            mlp_body(NG - 1)

        @block.vector
        def _(dve):
            def weight_lo(i, part):
                dve.wait_ge(w_hi_done[i], 1)
                dve.tensor_tensor(w_lo[i][:, part, :], raw_w[i][:, part], w_hi[i][:, part, :].bitcast(F32),
                                  ALU.subtract).then_inc(w_lo_done[i], 1)

            def ln_stats(g, par, t):
                if is_first(g):
                    dve.wait_ge(x0_loaded[t], 16)
                elif t == 0:
                    dve.wait_ge(x_loaded[par], 8 * (g + par))
                dve.bn_stats(stats[:, t, :], x[par][:, t, :]).then_inc(stats_done, 1)

            def ln_var(g):
                wait_apart(dve, stats_done, TILES * (g + 1), stats_passed)
                for t in range(TILES):
                    dve.bn_aggr(moments[:, t, :], stats[:, t, :]).then_inc(moments_done, 1)
                dve.wait_ge(moments_done, TILES * (g + 1))
                dve.tensor_scalar(var_eps[:, :], moments[:, :, 1], EPS, None, ALU.add).then_inc(var_done, 1)

            def ln_norm(g, par, t):
                dve.wait_ge(rstd_done, g + 1)
                dve.tensor_scalar(x[par][:, t, :], x[par][:, t, :], moments[:, t, 0:1], rstd[:, t:t + 1],
                                  ALU.subtract, ALU.mult).then_inc(zn_done, 1)

            def blocks_transposed(to, source, i, j):
                tokens, channels = (slice(q * BLK, (q + 1) * BLK) for q in (i, j))
                return dve.transpose(to[channels, :, :].rearrange("p k (t n) -> p t k n", n=P)[:, :, :, tokens],
                                     source[tokens, :, :].rearrange("p t (k n) -> p t k n", n=P)[:, :, :, channels])

            def ln_transpose(g, par, first, last):
                for n in range(first, last):
                    if n == 0:
                        dve.wait_ge(nx_split, KC * g)
                        wait_apart(dve, zn_done, TILES * (g + 1), zn_passed)
                    ins = blocks_transposed(z1T, x[par], n // QUADS, n % QUADS)
                    if n == QUADS * QUADS - 1:
                        ins.then_inc(z_transposed, 1)

            def nx_lo(g, k):
                if is_first(g):
                    dve.wait_ge(nx_done, KC * g + k + 1)
                    dve.tensor_copy(nxT_hi[:, k], z1T[:, k]).then_inc(nx_hi_done, 1)
                dve.wait_ge(nx_hi_done, KC * g + k + 1)
                dve.tensor_tensor(nxT_lo[:, k], z1T[:, k], nxT_hi[:, k].bitcast(F32),
                                  ALU.subtract).then_inc(nx_split, 1)

            def take_v(g, par, t, bank):
                dve.wait_ge(u_done, units_through(g, 3 * t + 2))
                dve.tensor_tensor(v[par][:, t, :], lin[bank][:, :], bv_all[:, :], ALU.add).then_inc(v_done, 1)

            def mask_and_shift(g, par, t):
                n = TILES * g + t
                if t == 0:
                    dve.wait_ge(mask_loaded[par], 8 * (g - par) + 16)
                dve.wait_ge(neg_filled, n + 1)
                wait_apart(dve, s_done, n + 1, mask_passed)
                flags = mask[:, par, t, :].unsqueeze(1).broadcast_to((P, HEADS, NODES))
                dve.copy_predicated(scores[:, t % 2], flags, ps_scores[:, t % 2]).then_inc(masked, 1)
                dve.wait_ge(masked, n + 1)
                dve.tensor_reduce(row_max[:, :], scores[:, t % 2], AX.X, ALU.max).then_inc(max_done, 1)
                dve.wait_ge(max_done, n + 1)
                dve.tensor_tensor(scores[:, t % 2], scores[:, t % 2],
                                  row_max[:, :].unsqueeze(2).broadcast_to((P, HEADS, NODES)),
                                  ALU.subtract).then_inc(shifted, 1)

            def normalise(g, t):
                n = TILES * g + t
                dve.wait_ge(exp_done, n + 1)
                dve.tensor_reduce(row_sum[:, :], expd[:, t % 2], AX.X, ALU.add).then_inc(sum_done, 1)
                dve.wait_ge(sum_done, n + 1)
                dve.reciprocal(row_inv[:, :], row_sum[:, :]).then_inc(inv_done, 1)
                dve.wait_ge(inv_done, n + 1)
                wait(dve, pt_done, n - 1)
                dve.tensor_tensor(prob[:, t % 2], expd[:, t % 2],
                                  row_inv[:, :].unsqueeze(2).broadcast_to((P, HEADS, NODES)),
                                  ALU.mult).then_inc(prob_done, 1)

            def att_lo(g, t):
                bank = bank_of(g, "O", t)
                n = TILES * g + t
                dve.wait_ge(att_hi_done, n + 1)
                dve.tensor_tensor(attT_lo[:, t % 2], lin[bank][:, :], attT_hi[:, t % 2].bitcast(F32),
                                  ALU.subtract).then_inc(att_split, 1)

            def residual(g, t):
                bank = bank_of(g, "W", t)
                n = TILES * g + t
                dve.wait_ge(proj_done, n + 1)
                dve.wait_ge(xres_biased, n + 1)
                dve.tensor_tensor(xres[:, t % 2], lin[bank][:, :], xres[:, t % 2], ALU.add).then_inc(x1_done, 1)

            def body(g, par):
                def unit_v(t):
                    if ("U", 3 * t + 2) in order_of(g):
                        take_v(g + 1, 1 - par, t, bank_of(g, "U", 3 * t + 2))
                ln = "N" in kinds_of(g)
                mask_and_shift(g, par, 0)
                if ln:
                    ln_stats(g + 2, par, 0)
                    ln_stats(g + 2, par, 1)
                normalise(g, 0)
                mask_and_shift(g, par, 1)
                unit_v(0)
                if ln:
                    ln_stats(g + 2, par, 2)
                    ln_stats(g + 2, par, 3)
                    ln_var(g + 2)
                normalise(g, 1)
                mask_and_shift(g, par, 2)
                att_lo(g, 0)
                if ln:
                    ln_norm(g + 2, par, 0)
                    ln_norm(g + 2, par, 1)
                unit_v(1)
                normalise(g, 2)
                mask_and_shift(g, par, 3)
                residual(g, 0)
                if ln:
                    ln_norm(g + 2, par, 2)
                    ln_norm(g + 2, par, 3)
                att_lo(g, 1)
                normalise(g, 3)
                if ln:
                    ln_transpose(g + 2, par, 0, 4)
                residual(g, 1)
                att_lo(g, 2)
                if ln:
                    ln_transpose(g + 2, par, 4, 5)
                unit_v(2)
                if ln:
                    ln_transpose(g + 2, par, 5, 12)
                residual(g, 2)
                att_lo(g, 3)
                if ln:
                    ln_transpose(g + 2, par, 12, 16)
                unit_v(3)
                if ln:
                    for k in range(KC):
                        nx_lo(g + 2, k)
                residual(g, 3)

            def last_body(g, par):
                def late_v(t):
                    take_v(g, par, t, bank_of(g, "L", 3 * t + 2))
                mask_and_shift(g, par, 0)
                normalise(g, 0)
                late_v(0)
                mask_and_shift(g, par, 1)
                late_v(1)
                mlp_ln_stats(0, 0, 0)
                mlp_ln_stats(0, 0, 1)
                normalise(g, 1)
                mask_and_shift(g, par, 2)
                late_v(2)
                mlp_ln_stats(0, 0, 2)
                mlp_ln_stats(0, 0, 3)
                att_lo(g, 0)
                normalise(g, 2)
                mask_and_shift(g, par, 3)
                late_v(3)
                mlp_ln_var(0)
                att_lo(g, 1)
                residual(g, 0)
                normalise(g, 3)
                for t in range(TILES):
                    mlp_ln_norm(0, 0, t)
                att_lo(g, 2)
                residual(g, 1)
                mlp_split_nx(0, 0)
                mlp_split_nx(0, 1)
                mlp_split_nx(0, 2)
                mlp_split_nx(0, 3)
                residual(g, 2)
                att_lo(g, 3)
                residual(g, 3)

            def mlp_ln_stats(g, par, t):
                if t == 0:
                    dve.wait_ge(x1_loaded[par], 8 * (g - par) + 16)
                dve.bn_stats(stats[:, t, :], x1[par][:, t, :]).then_inc(mlp_stats_done, 1)

            def mlp_ln_var(g):
                wait_apart(dve, mlp_stats_done, TILES * (g + 1), mlp_stats_passed)
                for t in range(TILES):
                    dve.bn_aggr(moments[:, t, :], stats[:, t, :]).then_inc(mlp_moments_done, 1)
                dve.wait_ge(mlp_moments_done, TILES * (g + 1))
                dve.tensor_scalar(var_eps[:, :], moments[:, :, 1], EPS, None, ALU.add).then_inc(mlp_var_done, 1)

            def mlp_ln_norm(g, par, t):
                dve.wait_ge(mlp_rstd_done, g + 1)
                if isinstance(g, int) and g == 1:
                    dve.wait_ge(first_t_done, KC)
                else:
                    wait(dve, mlp_t_done, g - 1)
                dve.tensor_scalar(zn[:, t, :], x1[par][:, t, :], moments[:, t, 0:1], rstd[:, t:t + 1],
                                  ALU.subtract, ALU.mult).then_inc(mlp_zn_done, 1)

            def mlp_transpose(g, n):
                if n == 0:
                    wait(dve, mlp_nx_split, KC * g)
                    wait_apart(dve, mlp_zn_done, TILES * (g + 1), zn_passed)
                ins = blocks_transposed(z2T, zn, n // QUADS, n % QUADS)
                if n == QUADS * QUADS - 1:
                    ins.then_inc(mlp_t_done, 1)

            def mlp_split_nx(g, k):
                dve.wait_ge(mlp_nx_done, KC * g + k + 1)
                wait(dve, up_done, FC * g)
                dve.tensor_copy(mlp_nxT_hi[:, k], z2T[:, k]).then_inc(mlp_nx_hi_done, 1)
                dve.wait_ge(mlp_nx_hi_done, KC * g + k + 1)
                dve.tensor_tensor(mlp_nxT_lo[:, k], z2T[:, k], mlp_nxT_hi[:, k].bitcast(F32),
                                  ALU.subtract).then_inc(mlp_nx_split, 1)

            def mlp_body(g, par):
                more = not isinstance(g, int) or g + 1 < NG
                for m in range(FC):
                    dve.wait_ge(h_hi_done, FC * g + m + 1)
                    dve.tensor_tensor(hT_lo[:, m % HR], hT[:, m % 2], hT_hi[:, m % HR].bitcast(F32),
                                      ALU.subtract).then_inc(h_split, 1)
                    if more and 2 <= m < 4:
                        for t in range(2 * (m - 2), 2 * (m - 1)):
                            mlp_ln_stats(g + 1, 1 - par, t)
                    if more and m == 4:
                        mlp_ln_var(g + 1)
                    if more and 5 <= m < 7:
                        for t in range(2 * (m - 5), 2 * (m - 4)):
                            mlp_ln_norm(g + 1, 1 - par, t)
                    if more and 7 <= m < 15:
                        for n in range(2 * (m - 7), 2 * (m - 6)):
                            mlp_transpose(g + 1, n)
                if more:
                    for k in range(KC):
                        mlp_split_nx(g + 1, k)
                for t in range(TILES):
                    if t < TILES - 1:
                        dve.wait_ge(tile_summed, (TILES - 1) * g + t + 1)
                    else:
                        dve.wait_ge(down_done, FC * (g + 1))
                    dve.wait_ge(x1_biased, TILES * g + t + 1)
                    dve.tensor_tensor(x1[par][:, t, :], ps_out[t][:, :], x1[par][:, t, :], ALU.add)\
                       .then_inc(out_done, 1)

            for g in range(2):
                for t in range(TILES):
                    ln_stats(g, g, t)
                ln_var(g)
                for t in range(TILES):
                    ln_norm(g, g, t)
                if g == 0:
                    weight_lo(0, slice(0, KC // 2))
                    for k in range(KC):
                        nx_lo(0, k)
                    weight_lo(2, slice(0, KC))
            weight_lo(3, slice(0, KC))
            dve.wait_ge(rows_loaded, 16 * 2)
            for t in range(TILES):
                take_v(0, 0, t, bank_of(-1, "U", 3 * t + 2))
            for k in range(KC):
                nx_lo(1, k)
            dve.wait_ge(w_lo_done[1], 1)
            dve.wait_ge(probT_zeroed, 2)
            body(0, 0)
            with dve.Fori(1, NG - 4, 2) as g:
                body(g, 1)
                body(g + 1, 0)
            for g in range(NG - 3, NG - 1):
                body(g, g % 2)
            last_body(NG - 1, 1)
            mlp_body(0, 0)
            with dve.Fori(1, NG - 2, 2) as g:
                mlp_body(g, 1)
                mlp_body(g + 1, 0)
            mlp_body(NG - 1, 1)

        @block.tensor
        def _(pe):
            def take_bank(g, kind, n):
                bank, last = ring_place(g, kind, n)
                if last is not None:
                    i, kind, n = last
                    which = {"U": (q_done, k_done, v_done)[n % 3], "L": v_done, "T": nx_done, "O": att_split,
                             "W": x1_done}[kind]
                    if kind == "L":
                        pe.wait_ge(v_done, KC * i + n // 3 + 1)
                    elif kind == "U":
                        per = 2 if n % 3 == 1 else 1
                        pe.wait_ge(which, per * (KC * (i + 1) + n // 3 + 1))
                    elif kind == "T":
                        pe.wait_ge(which, KC * (i + 2) + n + 1)
                    else:
                        pe.wait_ge(which, TILES * i + n + 1)
                return lin[bank]

            def transposes(g, par, k, bank):
                pe.wait_ge(zn_done, TILES * (g + 1))
                for t in range(TILES):
                    mm = pe.transpose(bank[:, t * P:(t + 1) * P], x[par][:, t, k * P:(k + 1) * P], ident[:, :])
                mm.then_inc(t_done, 1)

            def unit(g, j, bank):
                m, which = j // 3, j % 3
                if is_first(g) and m == 0:
                    pe.wait_ge(w_lo_done[which], 2 if which == 0 else 1)
                for c in range(KC):
                    if j == 0:
                        pe.wait_ge(nx_split, KC * g + c + 1)
                    nx = (nxT_hi[:, c, :], nxT_lo[:, c, :])
                    if which < 2:
                        lhs = tuple(w[which][:, c, m * P:(m + 1) * P] for w in (w_hi, w_lo))
                        rhs = nx
                    else:
                        lhs = tuple(n[:, m * P:(m + 1) * P] for n in nx)
                        rhs = tuple(w[2][:, c, :] for w in (w_hi, w_lo))
                    mm = split3(pe, bank[:, :], lhs, rhs, c == 0, c == KC - 1)
                mm.then_inc(u_done, 1)

            def score(g, par, t):
                n = TILES * g + t
                if t == 0:
                    pe.wait_ge(q_done, KC * (g + 1))
                    pe.wait_ge(k_done, 2 * KC * (g + 1))
                wait(pe, masked, n - 1)
                for m in range(KC):
                    for a in range(2):
                        mm = pe.matmul(ps_scores[a * NODES:(a + 1) * NODES, t % 2, 2 * m:2 * m + 2, :],
                                       qT[par][:, m, t * P + a * NODES:t * P + (a + 1) * NODES],
                                       kT[par][:, t, m, a, :, :], start=True, stop=True)
                mm.then_inc(s_done, 1)

            def prob_transposes(g, t):
                n = TILES * g + t
                pe.wait_ge(prob_done, n + 1)
                wait(pe, probT_done, 4 * (n - 1))
                for m in range(KC):
                    mm = pe.transpose(ps_probT[:, t % 2, m, :], prob[:, t % 2, 2 * m:2 * m + 2, :], ident[:, :])
                mm.then_inc(pt_done, 1)

            def attend(g, par, t, bank):
                pe.wait_ge(probT_done, 4 * (TILES * g + t + 1))
                if is_last(g):
                    pe.wait_ge(v_done, TILES * g + t + 1)
                elif t == 0:
                    pe.wait_ge(v_done, TILES * (g + 1))
                for h in range(HEADS):
                    rows = slice((h % 2) * HD, (h % 2 + 1) * HD)
                    mm = pe.matmul(bank[rows, (h // 2) * P:(h // 2 + 1) * P], v[par][:, t, h * HD:(h + 1) * HD],
                                   probT[:, t % 2, h // 2, h % 2, :, :], start=True, stop=True)
                mm.then_inc(o_done, 1)

            def project(g, t, bank):
                if is_first(g) and t == 0:
                    pe.wait_ge(w_lo_done[3], 1)
                pe.wait_ge(att_split, TILES * g + t + 1)
                for c in range(KC):
                    mm = split3(pe, bank[:, :], tuple(a[:, t % 2, c * P:(c + 1) * P] for a in (attT_hi, attT_lo)),
                                tuple(w[3][:, c, :] for w in (w_hi, w_lo)), c == 0, c == KC - 1)
                mm.then_inc(proj_done, 1)

            def body(g, par):
                for kind, n in order_of(g):
                    if kind == "S":
                        score(g, par, n)
                    elif kind == "P":
                        prob_transposes(g, n)
                    elif kind == "M":
                        first_transposes(n)
                    elif kind == "F":
                        pe.wait_ge(probT_done, 4 * (TILES * NG - 1))
                        up(0, 0)
                    elif kind == "L":
                        unit(g, n, take_bank(g, "L", n))
                    elif kind == "U":
                        unit(g + 1, n, take_bank(g, "U", n))
                    elif kind == "O":
                        attend(g, par, n, take_bank(g, "O", n))
                    elif kind == "W":
                        project(g, n, take_bank(g, "W", n))
                    else:
                        transposes(g + 2, par, n, take_bank(g, "T", n))

            def first_transposes(k):
                if k == 0:
                    pe.wait_ge(mlp_zn_done, TILES)
                    pe.wait_ge(masked, TILES * NG)
                wait(pe, mlp_nx_done, k - 1)
                for t in range(TILES):
                    mm = pe.transpose(ps_t[k % 2][:, t * P:(t + 1) * P], zn[:, t, k * P:(k + 1) * P], ident[:, :])
                mm.then_inc(first_t_done, 1)

            def up(g, m):
                n = FC * g + m
                wait(pe, gelu_done, n - 1)
                if is_first(g) and m % 2 == 0:
                    pe.wait_ge(piece_lo, PIECES.index((1, m // 2)) + 1)
                for c in range(KC):
                    if m == 0:
                        pe.wait_ge(mlp_nx_split, KC * g + c + 1)
                    mm = split3(pe, ps_h[m % 2][:, :], tuple(w[:, c, m * P:(m + 1) * P] for w in (w1_hi, w1_lo)),
                                (mlp_nxT_hi[:, c, :], mlp_nxT_lo[:, c, :]), c == 0, c == KC - 1)
                mm.then_inc(up_done, 1)

            def down(g, m):
                pe.wait_ge(h_split, FC * g + m + 1)
                if m == 0:
                    wait(pe, out_done, TILES * g)
                if m == 0 and is_first(g):
                    pe.wait_ge(x1_done, TILES * NG)
                if is_first(g) and m % 2 == 0:
                    pe.wait_ge(piece_lo, PIECES.index((2, m // 2)) + 1)
                for t in range(TILES):
                    mm = split3(pe, ps_out[t][:, :], tuple(h[:, m % HR, t * P:(t + 1) * P] for h in (hT_hi, hT_lo)),
                                (w2_hi[:, m, :], w2_lo[:, m, :]), m == 0, m == FC - 1)
                    if m == FC - 1 and t < TILES - 1:
                        mm.then_inc(tile_summed, 1)
                mm.then_inc(down_done, 1)

            def mlp_body(g):
                for m in range(FC):
                    if not (is_first(g) and m == 0):
                        up(g, m)
                    if m >= LAG:
                        down(g, m - LAG)
                for m in range(FC - LAG, FC):
                    down(g, m)

            pe.wait_ge(ident_done, 1)
            for t in range(TILES):
                pe.wait_ge(zn_done, t + 1)
                for k in range(KC):
                    mm = pe.transpose(lin[bank_of(-2, "T", k)][:, t * P:(t + 1) * P], x[0][:, t, k * P:(k + 1) * P],
                                      ident[:, :])
                    if t == TILES - 1:
                        mm.then_inc(t_done, 1)
            body(-1, 1)
            body(0, 0)
            with pe.Fori(1, NG - 4, 2) as g:
                body(g, 1)
                body(g + 1, 0)
            for g in range(NG - 3, NG):
                body(g, g % 2)
            pe.wait_ge(probT_done, 4 * TILES * NG)
            mlp_body(0)
            with pe.Fori(1, NG - 2, 2) as g:
                mlp_body(g)
                mlp_body(g + 1)
            mlp_body(NG - 1)


_INS = ["x", "adj"] + [f"L0_gnn_{n}" for n in ("ln1_g", "ln1_b", "ln2_g", "ln2_b", "Wq", "bq", "Wk", "bk", "Wv", "bv",
                                               "Wo", "bo", "W1", "b1", "W2", "b2")]


def kernel(**inputs):
    import numpy as np
    import concourse.bacc as bacc
    from concourse.bass_utils import run_bass_kernel_spmd

    nc = bacc.Bacc("TRN2", target_bir_lowering=False, num_devices=1)
    arrays, args = {}, []
    for name in _INS:
        a = np.ascontiguousarray(inputs[name])
        if name == "x":
            a = a.reshape(TOKENS, HID)
        arrays[f"in_{name}"] = a
        args.append(nc.dram_tensor(f"in_{name}", a.shape, mybir.dt.from_np(a.dtype), kind="ExternalInput").ap())
    out = nc.dram_tensor("out", (TOKENS, HID), F32, kind="ExternalOutput").ap()
    adj_layer(nc, *args, out)
    r = run_bass_kernel_spmd(nc, [arrays], core_ids=[0])
    return r.results[0]["out"].reshape(GRAPHS, NODES, HID)
```
